# Optimizing a Trainium2 kernel written in Bass

```python
import numpy as np
import jax
import jax.numpy as jnp

def _softmax(x, axis=-1):
    return jax.nn.softmax(x, axis=axis)

def _gelu(x):
    return jax.nn.gelu(x, approximate=True)

def _silu(x):
    return jax.nn.silu(x)

def _sigmoid(x):
    return jax.nn.sigmoid(x)

def _layernorm(x, axis=-1, eps=1e-05):
    m = jnp.mean(x, axis=axis, keepdims=True)
    v = jnp.var(x, axis=axis, keepdims=True)
    return (x - m) / jnp.sqrt(v + eps)

def _scatter_add(tgt, idx, src, axis=0):
    return tgt.at[idx].add(src)

def _segment_sum(src, seg, n):
    return jax.ops.segment_sum(src, seg, n)
kernel_name = 'mk_recurrent_d1_jaxref_r8_0623eb'

def setup_inputs(seed: int=0):
    np.random.seed(seed)
    _w = jnp.asarray

    def _L0_attn_setup():
        import jax, jax.numpy as jnp
        import numpy as np
        B, S, H = (8, 128, 128)
        HEADS = 8
        HD = H // HEADS
        LAMBDA_INIT = 0.8
        LN_EPS = 1e-05
        key = jax.random.key(seed)
        ks = jax.random.split(key, 16)
        xavier = float(np.sqrt(6.0 / (H + H)))
        inp = {'hidden_states': jax.random.normal(ks[0], (B, S, H), dtype=jnp.float32), 'Wq': jax.random.uniform(ks[1], (H, H), jnp.float32, -xavier, xavier), 'bq': jnp.zeros((H,), jnp.float32), 'Wk': jax.random.uniform(ks[2], (H, H), jnp.float32, -xavier, xavier), 'bk': jnp.zeros((H,), jnp.float32), 'Wv': jax.random.uniform(ks[3], (H, H), jnp.float32, -xavier, xavier), 'bv': jnp.zeros((H,), jnp.float32), 'Wo': jax.random.uniform(ks[4], (H, H), jnp.float32, -xavier, xavier), 'bo': jnp.zeros((H,), jnp.float32), 'lambda_q1': 0.02 * jax.random.normal(ks[5], (HD,), jnp.float32), 'lambda_k1': 0.02 * jax.random.normal(ks[6], (HD,), jnp.float32), 'lambda_q2': 0.02 * jax.random.normal(ks[7], (HD,), jnp.float32), 'lambda_k2': 0.02 * jax.random.normal(ks[8], (HD,), jnp.float32), 'ln_w': jnp.ones((H,), jnp.float32), 'ln_b': jnp.zeros((H,), jnp.float32)}
        return inp
    _L0_attn_in = _L0_attn_setup()

    def _L0_ffn_setup():
        import jax, jax.numpy as jnp
        import numpy as np
        HIDDEN = 128
        NUM_EXPERTS = 8
        TOP_K = 2
        B, S = (2, 256)
        key = jax.random.key(seed)
        k1, k2, k3, k4, k5 = jax.random.split(key, 5)
        d, dff, E = (HIDDEN, 4 * HIDDEN, NUM_EXPERTS)
        x = jax.random.normal(k1, (B, S, d), dtype=jnp.float32)
        W1 = jax.random.normal(k2, (E, d, dff), dtype=jnp.float32) * (1.0 / np.sqrt(d))
        b1 = jax.random.normal(k3, (E, dff), dtype=jnp.float32) * 0.01
        W2 = jax.random.normal(k4, (E, dff, d), dtype=jnp.float32) * (1.0 / np.sqrt(dff))
        b2 = jax.random.normal(k5, (E, d), dtype=jnp.float32) * 0.01
        return {'x': x, 'W1': W1, 'b1': b1, 'W2': W2, 'b2': b2}
    _L0_ffn_in = _L0_ffn_setup()
    _d = {'L0_attn_hidden_states': _L0_attn_in['hidden_states'], 'L0_attn_Wq': _L0_attn_in['Wq'], 'L0_attn_bq': _L0_attn_in['bq'], 'L0_attn_Wk': _L0_attn_in['Wk'], 'L0_attn_bk': _L0_attn_in['bk'], 'L0_attn_Wv': _L0_attn_in['Wv'], 'L0_attn_bv': _L0_attn_in['bv'], 'L0_attn_Wo': _L0_attn_in['Wo'], 'L0_attn_bo': _L0_attn_in['bo'], 'L0_attn_lambda_q1': _L0_attn_in['lambda_q1'], 'L0_attn_lambda_k1': _L0_attn_in['lambda_k1'], 'L0_attn_lambda_q2': _L0_attn_in['lambda_q2'], 'L0_attn_lambda_k2': _L0_attn_in['lambda_k2'], 'L0_attn_ln_w': _L0_attn_in['ln_w'], 'L0_attn_ln_b': _L0_attn_in['ln_b'], 'L0_ffn_W1': _L0_ffn_in['W1'], 'L0_ffn_b1': _L0_ffn_in['b1'], 'L0_ffn_W2': _L0_ffn_in['W2'], 'L0_ffn_b2': _L0_ffn_in['b2']}
    _x0 = _d['L0_attn_hidden_states']
    _d['L0_attn_hidden_states'] = jax.random.normal(jax.random.fold_in(jax.random.key(seed), 1), (8, 512, 128), dtype=_x0.dtype)
    del _x0
    return _d

def reference(L0_attn_hidden_states, L0_attn_Wq, L0_attn_bq, L0_attn_Wk, L0_attn_bk, L0_attn_Wv, L0_attn_bv, L0_attn_Wo, L0_attn_bo, L0_attn_lambda_q1, L0_attn_lambda_k1, L0_attn_lambda_q2, L0_attn_lambda_k2, L0_attn_ln_w, L0_attn_ln_b, L0_ffn_W1, L0_ffn_b1, L0_ffn_W2, L0_ffn_b2):

    def _L0_attn_ref(hidden_states, Wq, bq, Wk, bk, Wv, bv, Wo, bo, lambda_q1, lambda_k1, lambda_q2, lambda_k2, ln_w, ln_b):
        import jax, jax.numpy as jnp
        import numpy as np
        B, S, H = (8, 128, 128)
        HEADS = 8
        HD = H // HEADS
        LAMBDA_INIT = 0.8
        LN_EPS = 1e-05
        b, s, h = hidden_states.shape
        q = hidden_states @ Wq + bq
        k = hidden_states @ Wk + bk
        v = hidden_states @ Wv + bv
        q = q.reshape(b, s, HEADS, HD).transpose(0, 2, 1, 3)
        k = k.reshape(b, s, HEADS, HD).transpose(0, 2, 1, 3)
        v = v.reshape(b, s, HEADS, HD).transpose(0, 2, 1, 3)
        scores = jnp.einsum('bhqd,bhkd->bhqk', q, k) / jnp.sqrt(jnp.float32(HD))
        attn = jax.nn.softmax(scores, axis=-1)
        half = HEADS // 2
        v1 = jnp.concatenate([v[:, :half], v[:, :half]], axis=1)
        v2 = jnp.concatenate([v[:, half:], v[:, half:]], axis=1)
        out1 = jnp.einsum('bhqk,bhkd->bhqd', attn, v1)
        out2 = jnp.einsum('bhqk,bhkd->bhqd', attn, v2)
        lam1 = jnp.exp(jnp.sum(lambda_q1 * lambda_k1))
        lam2 = jnp.exp(jnp.sum(lambda_q2 * lambda_k2))
        lam = lam1 - lam2 + LAMBDA_INIT
        attn_out = out1 - lam * out2
        attn_out = attn_out.transpose(0, 2, 1, 3).reshape(b, s, h)
        mu = jnp.mean(attn_out, axis=-1, keepdims=True)
        var = jnp.var(attn_out, axis=-1, keepdims=True)
        normed = (attn_out - mu) / jnp.sqrt(var + LN_EPS) * ln_w + ln_b
        attn_out = (1.0 - LAMBDA_INIT) * normed
        return attn_out @ Wo + bo

    def _L0_ffn_ref(x, W1, b1, W2, b2):
        import jax, jax.numpy as jnp
        import numpy as np
        HIDDEN = 128
        NUM_EXPERTS = 8
        TOP_K = 2
        B, S = (2, 256)
        Bm, Sm, d = x.shape
        E = W1.shape[0]
        x_flat = x.reshape(-1, d)
        h = jnp.mod(x_flat[:, :TOP_K].sum(axis=1).astype(jnp.int32), E)
        sel = jnp.stack([h, jnp.mod(h + 1, E)], axis=1)

        def step(acc, params):
            e, W1e, b1e, W2e, b2e = params
            w = jnp.any(sel == e, axis=1).astype(x.dtype) / TOP_K
            y = jnp.maximum(x_flat @ W1e + b1e, 0.0) @ W2e + b2e
            return (acc + w[:, None] * y, None)
        init = jnp.zeros_like(x_flat)
        out_flat, _ = jax.lax.scan(step, init, (jnp.arange(E), W1, b1, W2, b2))
        return out_flat.reshape(Bm, Sm, d)
    x = L0_attn_hidden_states
    xn = _layernorm(x, axis=-1)
    s = _L0_attn_ref(xn, L0_attn_Wq, L0_attn_bq, L0_attn_Wk, L0_attn_bk, L0_attn_Wv, L0_attn_bv, L0_attn_Wo, L0_attn_bo, L0_attn_lambda_q1, L0_attn_lambda_k1, L0_attn_lambda_q2, L0_attn_lambda_k2, L0_attn_ln_w, L0_attn_ln_b)
    g = _silu(_L0_ffn_ref(xn, L0_ffn_W1, L0_ffn_b1, L0_ffn_W2, L0_ffn_b2))
    x = x + s * g
    return x

_drawn_inputs = setup_inputs


def setup_inputs(seed=0):
    import zlib

    import numpy as np

    out = dict(_drawn_inputs(seed))
    spreads = {'L0_attn_bq': (0.0, 0.8),
     'L0_attn_bk': (0.0, 2.0),
     'L0_attn_bv': (0.0, 0.1),
     'L0_attn_bo': (0.0, 0.301),
     'L0_attn_ln_w': (1.0, 0.6),
     'L0_attn_ln_b': (0.0, 0.8)}
    factors = {'L0_attn_lambda_q1': 64.0,
     'L0_attn_lambda_k1': 45.911,
     'L0_attn_lambda_q2': 64.0,
     'L0_attn_lambda_k2': 64.0,
     'L0_ffn_b1': 42.798,
     'L0_ffn_b2': 31.351}
    for name, (base, spread) in spreads.items():
        noise = np.random.default_rng([zlib.crc32(name.encode()), seed]).standard_normal(out[name].shape)
        drawn = base * np.exp(spread * noise) if base else spread * noise
        out[name] = jnp.asarray(drawn.astype(out[name].dtype))
    for name, factor in factors.items():
        out[name] = (out[name] * factor).astype(out[name].dtype)
    return out
```

```python
import concourse.bass as bass
from concourse import mybir
from contextlib import ExitStack

F32 = mybir.dt.float32
BF16 = mybir.dt.bfloat16
I32 = mybir.dt.int32
ALU = mybir.AluOpType
ACT = mybir.ActivationFunctionType
AX = mybir.AxisListType

P = 128
B, S, D = 8, 512, 128
HEADS, HD = 8, 16
HALF = HEADS // 2
C = S // P
NT = B * C
EXP = 8
FF = 4 * D
FC = FF // P
FT = NT + (EXP * (P - 1)) // P
LAM_INIT = 0.8
OUT_SCALE = 1.0 - LAM_INIT
EPS = 1e-5
SCALE = 1.0 / HD ** 0.5
PARTS = 3
Q_PART = [0, 1, 2, 0, 1, 0]
K_PART = [0, 0, 0, 1, 1, 2]
MAX_ROW = len(Q_PART) * HD
KROWS = MAX_ROW + PARTS
VW = 32
XB = 3
STK = 3
PR = 8
T_B2, T_W1, T_B1 = 0, D, D + FF
TW = D + FF + FC
WB = 2


def schedule():
    steps = []

    def at(time, *step):
        steps.append((time, len(steps), step))

    for b in range(B):
        at(-30 + 0.5 * b if b < XB else -21 + b, "load_x", b)
        at(-22 if b == 0 else -21 + b, "norm", b)
        qkv = -21.5 if b == 0 else 32 * b - 20
        at(qkv, "transpose_x", b)
        at(qkv + 1 if b else -21.4, "project", b, 0)
        at(qkv + 3 if b else -21.3, "project", b, 1)
        at(32 * b + 12.6 if b >= 2 else qkv + 5 if b else -21.2, "values", b)
        at(qkv + 6 if b else -21.1, "stack", b)
        for n in range(32 * b, 32 * b + 32):
            at(n, "score", n)
            at(n + 40, "exp", n)
            if n % 4 == 3:
                at(n + 43.5, "pv", n // 4)
        at(32 * b + 32.3, "row_max", b)
        for grp in (2 * b, 2 * b + 1):
            at(16 * grp + 60, "copy_o", grp)
            at(16 * grp + 62.2, "turn_o", grp)
        at(32 * b + 80.1, "norm_o", b)
        at(32 * b + 84.3, "turn_z", b)
        at(32 * b + 86.3, "project_o", b)
        at(max(32 * b + 88, 286 + b), "finish", b)
    at(-12, "route")
    at(-11, "scatter")
    f0, pace = 30.0, 5.6
    for f in range(FT):
        t = f0 + pace * f
        at(t - 6, "load_tile", f)
        at(t - 1.1, "turn_tile", f)
        at(t, "hidden", f, 0)
        at(t + 2.2, "hidden", f, 1)
        at(t + 4.6, "down", f)
        at(t + 5.5, "store_tile", f)
    end = f0 + pace * FT
    at(end + 1.5, "gather")
    at(end + 35, "gate")
    return [s for _, _, s in sorted(steps)]


def gated_attention_moe(nc, x, wq, bq, wk, bk, wv, bv, wo, bo, lq1, lk1, lq2, lk2,
                        ln_w, ln_b, w1, b1, w2, b2, out):
    steps = schedule()
    uses = {}
    for s in steps:
        if s[0] in ("transpose_x", "project", "values", "row_max", "turn_o", "turn_z", "project_o",
                    "route", "turn_tile", "down"):
            uses[s] = len(uses) + 1

    x_v = x.rearrange("b (c p) d -> b p c d", p=P)
    out_v = out.rearrange("b (c p) d -> b p c d", p=P)
    sorted_x = nc.dram_tensor("sorted_x", (FT * P, D), F32, kind="Internal").ap()
    sorted_y = nc.dram_tensor("sorted_y", (FT * P, D), F32, kind="Internal").ap()

    ctx = ExitStack()
    with ctx:
        def sb(name, shape, dt=F32):
            return ctx.enter_context(nc.sbuf_tensor(name, shape, dt))

        def bank(name):
            return ctx.enter_context(nc.psum_tensor(name, [P, 512], F32))

        def sem(name):
            return ctx.enter_context(nc.semaphore(name))

        ident = sb("ident", [P, P])
        before = sb("before", [P, P])
        ones = sb("ones", [P, P])
        iota_i = sb("iota_i", [P, 40], I32)
        iota = sb("iota", [P, 40])
        neg_half = sb("neg_half", [P, C])
        wq_sb = sb("wq_sb", [P, D])
        wk_sb = sb("wk_sb", [P, D])
        wv_sb = sb("wv_sb", [P, D])
        wo_sb = sb("wo_sb", [P, D])
        wqk = sb("wqk", [P, 2, D])
        qk_bias = sb("qk_bias", [P, 2])
        bv_sb = sb("bv_sb", [P, D])
        bo_sb = sb("bo_sb", [P, D])
        lams = sb("lams", [P, 4, HD])
        lam_prod = sb("lam_prod", [P, 2, HD])
        lam_dot = sb("lam_dot", [P, 2])
        lam_exp = sb("lam_exp", [P, 2])
        neg_lam = sb("neg_lam", [P, 1])
        lnw_sb = sb("lnw_sb", [P, 1])
        lnb_sb = sb("lnb_sb", [P, 1])
        lnb_wide = sb("lnb_wide", [P, P])
        wv_eff = sb("wv_eff", [P, HALF * HD])
        bv_eff = sb("bv_eff", [P, HALF * HD])
        wo_eff = sb("wo_eff", [P, D])
        bo_eff = sb("bo_eff", [P, D])
        table = sb("table", [P, (EXP + 1) * TW])
        w2_sb = sb("w2_sb", [P, (EXP + 1) * FF])
        xn = sb("xn", [P, NT, D])
        yg = xn
        xin = sb("xin", [P, XB, C, D])
        stats = sb("stats", [P, C, 6])
        mv = sb("mv", [P, 2, C, 2])
        var_eps = sb("var_eps", [P, C])
        rstd = sb("rstd", [P, 2, C])
        shift = sb("shift", [P, 2, C])
        xT = sb("xT", [P, 2, S])
        parts = sb("parts", [P, 2, PARTS, S], BF16)
        rest = sb("rest", [P, S])
        qs = sb("qs", [P, STK, HEADS, S], BF16)
        ks = sb("ks", [P, STK, HEADS, S], BF16)
        va = sb("va", [P, 2, C, HALF, VW])
        neg_max = sb("neg_max", [P, 2, HEADS * C])
        max_parts = sb("max_parts", [HEADS * C, PARTS, P], BF16)
        max_rest = sb("max_rest", [HEADS * C, P])
        probs = sb("probs", [P, PR, S])
        oT = sb("oT", [P, 2, S])
        inv_sum = sb("inv_sum", [P, C * HALF])
        attn = sb("attn", [P, 2, C, D])
        stats_o = sb("stats_o", [P, C, 6])
        mv_o = sb("mv_o", [P, C, 2])
        var_eps_o = sb("var_eps_o", [P, C])
        rstd_o = sb("rstd_o", [P, C])
        shift_o = sb("shift_o", [P, C])
        z = sb("z", [P, C, D])
        zT = sb("zT", [P, S])
        s_sb = sb("s_sb", [P, NT, D])
        b2_sb = s_sb[:, 0:EXP + 1, :]
        x_again = xin
        v01 = sb("v01", [P, NT])
        v_abs = sb("v_abs", [P, NT])
        n_abs = sb("n_abs", [P, NT])
        sign = sb("sign", [P, NT])
        h = sb("h", [P, NT])
        wrap = sb("wrap", [P, 3, NT])
        count = sb("count", [P, EXP])
        tiles_of = sb("tiles_of", [P, EXP])
        tile_end = sb("tile_end", [P, EXP])
        tile_base = sb("tile_base", [P, EXP])
        base = sb("base", [P, EXP])
        slot_f = sb("slot_f", [P, NT])
        slot = sb("slot", [P, NT], I32)
        texp_f = sb("texp_f", [P, FT])
        texp = sb("texp", [P, FT], I32)
        xs = sb("xs", [P, 2, D])
        xsT = sb("xsT", [P, 2, P])
        pair = sb("pair", [P, WB, 2 * TW])
        hT = sb("hT", [P, 2, 2 * FC, P])
        work = hT[:, :, :, :].rearrange("p a k n -> p (a k n)")
        cmp = work[:, 0:512]
        onehot = work[:, 512:768].rearrange("p (e t) -> p e t", e=EXP)
        seen = work[:, 768:1024].rearrange("p (e t) -> p e t", e=EXP)
        zeros = work[:, 1024:1024 + EXP * NT]
        y_sb = sb("y_sb", [P, 2, D])

        score_bank = [bank("score0"), bank("score1")]
        exp_bank = [bank("exp0"), bank("exp1")]
        pv_bank = bank("pv_bank")
        hid_bank = [bank("hid0"), bank("hid1")]
        shared = bank("shared")

        consts_ready = sem("consts_ready")
        iota_ready = sem("iota_ready")
        ident_zero = sem("ident_zero")
        dve_consts = sem("dve_consts")
        small_loaded = sem("small_loaded")
        expert_loaded = sem("expert_loaded")
        lam_dots = sem("lam_dots")
        lam_exps = sem("lam_exps")
        folded = sem("folded")
        lnb_ready = sem("lnb_ready")
        table_ready = sem("table_ready")
        x_loaded = [sem(f"x_loaded{b}") for b in range(B)]
        x_reloaded = [sem(f"x_reloaded{b}") for b in range(B)]
        stats_ready = sem("stats_ready")
        rstd_ready = sem("rstd_ready")
        xn_ready = sem("xn_ready")
        shared_filled = sem("shared_filled")
        shared_free = sem("shared_free")
        xT_ready = sem("xT_ready")
        high_ready = sem("high_ready")
        rest_ready = sem("rest_ready")
        mid_ready = sem("mid_ready")
        low_ready = sem("low_ready")
        stacked = [sem(f"stacked{i}") for i in range(STK)]
        parts_sent = sem("parts_sent")
        va_ready = sem("va_ready")
        score_filled = sem("score_filled")
        max_taken = sem("max_taken")
        max_split = sem("max_split")
        max_stacked = sem("max_stacked")
        exp_filled = sem("exp_filled")
        exp_done = sem("exp_done")
        pv_done = sem("pv_done")
        o_copied = sem("o_copied")
        attn_ready = sem("attn_ready")
        stats_o_ready = sem("stats_o_ready")
        z_ready = sem("z_ready")
        zT_ready = sem("zT_ready")
        s_ready = sem("s_ready")
        sorted_zeroed = sem("sorted_zeroed")
        slots_ready = sem("slots_ready")
        count_ready = sem("count_ready")
        texp_ready = sem("texp_ready")
        scattered = sem("scattered")
        tile_loaded = [sem(f"tile_loaded{i}") for i in range(2)]
        pair_loaded = [sem(f"pair_loaded{i}") for i in range(WB)]
        xsT_ready = sem("xsT_ready")
        hid_filled = [sem(f"hid_filled{j}") for j in range(2)]
        hid_ready = [sem(f"hid_ready{j}") for j in range(2)]
        y_ready = sem("y_ready")
        y_stored = [sem(f"y_stored{i}") for i in range(2)]
        gathered = [sem(f"gathered{b}") for b in range(B)]
        gate_ready = sem("gate_ready")
        out_ready = sem("out_ready")
        out_stored = sem("out_stored")
        dve_chain = sem("dve_chain")
        pool_chain = sem("pool_chain")
        act_chain = sem("act_chain")

        block = ctx.enter_context(nc.Block())

        def row(ap):
            return ap.rearrange("(a n) -> a n", a=1)

        SMALL = 10

        @block.sync
        def _(sp):
            def load_x(b):
                if b >= XB:
                    sp.wait_ge(xn_ready, b - XB + 1)
                sp.dma_start(xin[:, b % XB, :, :], x_v[b]).then_inc(x_loaded[b], 16)

            load_x(0)
            sp.dma_start(wq_sb[:, :], wq).then_inc(small_loaded, 16)
            sp.dma_start(wk_sb[:, :], wk).then_inc(small_loaded, 16)
            sp.dma_start(wv_sb[:, :], wv).then_inc(small_loaded, 16)
            sp.dma_start(wo_sb[:, :], wo).then_inc(small_loaded, 16)
            sp.dma_start(bv_sb[:, :], row(bv).to_broadcast([P, D])).then_inc(small_loaded, 16)
            sp.dma_start(bo_sb[:, :], row(bo).to_broadcast([P, D])).then_inc(small_loaded, 16)
            for i, v in enumerate((bq, bk)):
                if True:
                    sp.dma_start(qk_bias[:, i:i + 1], v.rearrange("(h d) -> d h", d=HD),
                                 allow_slow_non_contiguous=True).then_inc(small_loaded, 16)
            sp.dma_start(lnw_sb[:, :], ln_w.rearrange("(p a) -> p a", a=1)).then_inc(small_loaded, 16)
            sp.dma_start(lnb_sb[:, :], ln_b.rearrange("(p a) -> p a", a=1)).then_inc(small_loaded, 16)
            load_x(1)
            load_x(2)

            for s in steps:
                kind = s[0]
                if kind == "load_x" and s[1] >= XB:
                    load_x(s[1])
                elif kind == "stack":
                    b = s[1]
                    sp.wait_ge(low_ready, 2 * b + 2)
                    if b >= STK:
                        sp.wait_ge(exp_done, 32 * (b - STK + 1))
                    for i, (dst, order) in enumerate(((qs, Q_PART), (ks, K_PART))):
                        for blk, part in enumerate(order):
                            sp.dma_start(dst[blk * HD:(blk + 1) * HD, b % STK, :, :],
                                         parts[:, i, part, :]).then_inc(stacked[b % STK], 16)
                elif kind == "row_max":
                    b = s[1]
                    sp.wait_ge(max_split, b + 1)
                    for part in range(PARTS):
                        sp.dma_start(qs[MAX_ROW + part:MAX_ROW + part + 1, b % STK, :, :],
                                     max_parts[:, part, :]).then_inc(max_stacked, 16)
                elif kind == "load_tile":
                    f = s[1]
                    if f == 0:
                        sp.wait_ge(scattered, 16 * NT)
                        sp.wait_ge(texp_ready, 1)
                        sp.wait_ge(table_ready, 1)
                    if f >= 2:
                        sp.wait_ge(xsT_ready, f - 1)
                    sp.dma_start(xs[:, f % 2, :], sorted_x[f * P:(f + 1) * P, :]).then_inc(tile_loaded[f % 2], 16)
                    if f >= WB:
                        sp.wait_ge(y_ready, f - WB + 1)
                    e = sp.value_load(texp[0:1, f:f + 1], min_val=0, max_val=EXP - 1)
                    sp.dma_start(pair[:, f % WB, :], table[:, bass.ds(e * TW, 2 * TW)]).then_inc(pair_loaded[f % WB], 16)
                elif kind == "store_tile":
                    f = s[1]
                    sp.wait_ge(y_ready, f + 1)
                    sp.dma_start(sorted_y[f * P:(f + 1) * P, :], y_sb[:, f % 2, :]).then_inc(y_stored[f % 2], 16)
                elif kind == "finish":
                    b = s[1]
                    if b == 0:
                        for bb in range(2):
                            sp.dma_start(x_again[:, bb, :, :], x_v[bb]).then_inc(x_reloaded[bb], 16)
                    sp.wait_ge(out_ready, b + 1)
                    sp.dma_start(out_v[b], s_sb[:, C * b:C * b + C, :]).then_inc(out_stored, 16)
                    if b + 2 < B:
                        sp.dma_start(x_again[:, b % 2, :, :], x_v[b + 2]).then_inc(x_reloaded[b + 2], 16)
            sp.wait_ge(out_stored, 16 * B)

        @block.gpsimd
        def _(pool):
            chain = [0]

            def link(ins):
                chain[0] += 1
                ins.then_inc(pool_chain, 1)
                pool.wait_ge(pool_chain, chain[0])

            g = nc.gpsimd
            link(g.memset(ident[:, :], 0.0))
            link(g.affine_select(out=ident[:, :], in_=ident[:, :], compare_op=ALU.not_equal, fill=1.0,
                                 base=0, pattern=[[-1, P]], channel_multiplier=1))
            link(g.memset(ones[:, :], 1.0))
            link(g.affine_select(out=before[:, :], in_=ones[:, :], compare_op=ALU.is_gt, fill=0.0,
                                 base=0, pattern=[[1, P]], channel_multiplier=-1))
            g.memset(neg_half[:, :], -0.5).then_inc(consts_ready, 1)
            link(g.iota(iota_i[:, :], pattern=[[1, 40]], base=0, channel_multiplier=0))
            g.tensor_copy(iota[:, :], iota_i[:, :]).then_inc(iota_ready, 1)
            tab = table[:, :].rearrange("p (e w) -> p e w", e=EXP + 1)
            w2v = w2_sb[:, :].rearrange("p (e w) -> p e w", e=EXP + 1)

            def load_experts():
                for e0, n, src in ((0, EXP, 0), (EXP, 1, 0)):
                    pool.dma_start(tab[:, e0:e0 + n, T_W1:T_W1 + FF],
                                   w1[src:src + n].rearrange("e p n -> p e n")).then_inc(expert_loaded, 16)
                    pool.dma_start(b2_sb[:, e0:e0 + n, :].rearrange("p e d -> p (e d)"),
                                   row(b2[src:src + n].rearrange("e d -> (e d)")).to_broadcast([P, n * D])).then_inc(expert_loaded, 16)
                    for e in range(n):
                        pool.dma_start(tab[:, e0 + e, T_B1:T_B1 + FC],
                                       b1[src + e].rearrange("(c p) -> p c", p=P),
                                       allow_slow_non_contiguous=True).then_inc(expert_loaded, 16)
                        pool.dma_start(w2v[:, e0 + e, :].rearrange("p (c n) -> p c n", c=FC),
                                       w2[src + e].rearrange("(c p) n -> p c n", p=P)).then_inc(expert_loaded, 16)

            for s in steps:
                kind = s[0]
                if kind == "norm":
                    b = s[1]
                    if b == 0:
                        pool.wait_ge(consts_ready, 1)
                    pool.wait_ge(stats_ready, b + 1)
                    if b >= 2:
                        pool.wait_ge(xn_ready, b - 1)
                    link(g.tensor_scalar(var_eps[:, :], mv[:, b % 2, :, 1], EPS, None, ALU.add))
                    link(g.tensor_tensor(rstd[:, b % 2, :], var_eps[:, :], neg_half[:, :], ALU.pow))
                    link(g.tensor_scalar(shift[:, b % 2, :], mv[:, b % 2, :, 0], -1.0, None, ALU.mult))
                    g.tensor_tensor(shift[:, b % 2, :], shift[:, b % 2, :], rstd[:, b % 2, :],
                                    ALU.mult).then_inc(rstd_ready, 1)
                elif kind == "project":
                    b, i = s[1:]
                    n = 2 * b + i
                    pool.wait_ge(rest_ready, n + 1)
                    if b >= 1:
                        pool.wait_ge(stacked[(b - 1) % STK], 12 * 16 * ((b - 1) // STK + 1))
                    g.tensor_copy(parts[:, i, 1, :], rest[:, :]).then_inc(mid_ready, 1)
                    pool.wait_ge(mid_ready, n + 1)
                    g.tensor_tensor(parts[:, i, 2, :], rest[:, :], parts[:, i, 1, :],
                                    ALU.subtract).then_inc(low_ready, 1)
                    if n == 1:
                        load_experts()
                elif kind == "norm_o":
                    b = s[1]
                    pool.wait_ge(stats_o_ready, b + 1)
                    if b >= 1:
                        pool.wait_ge(shared_filled, uses[("turn_z", b - 1)] + 1)
                    link(g.tensor_scalar(var_eps_o[:, :], mv_o[:, :, 1], EPS, None, ALU.add))
                    link(g.tensor_tensor(rstd_o[:, :], var_eps_o[:, :], neg_half[:, :], ALU.pow))
                    link(g.tensor_scalar(shift_o[:, :], mv_o[:, :, 0], -1.0, None, ALU.mult))
                    link(g.tensor_tensor(shift_o[:, :], shift_o[:, :], rstd_o[:, :], ALU.mult))
                    for c in range(C):
                        last = g.tensor_scalar(z[:, c, :], attn[:, b % 2, c, :], rstd_o[:, c:c + 1],
                                               shift_o[:, c:c + 1], ALU.mult, ALU.add)
                    last.then_inc(z_ready, 1)
                elif kind == "route":
                    g.memset(xs[:, :, :], 0.0).then_inc(ident_zero, 1)
                    pool.wait_ge(ident_zero, 1)
                    pool.dma_start(sorted_x.rearrange("(f p) d -> p f d", p=P),
                                   xs[:, 0:1, :].to_broadcast([P, FT, D])).then_inc(sorted_zeroed, 16)
                elif kind == "scatter":
                    pool.wait_ge(sorted_zeroed, 16)
                    pool.wait_ge(slots_ready, 1)
                    pool.wait_ge(xn_ready, B)
                    for t in range(NT):
                        pool.indirect_dma_start(
                            sorted_x, bass.IndirectOffsetOnAxis(ap=slot[:, t:t + 1], axis=0),
                            xn[:, t, :], None).then_inc(scattered, 16)
                elif kind == "gather":
                    for i in range(2):
                        pool.wait_ge(y_stored[i], 16 * len(range(i, FT, 2)))
                    pool.wait_ge(scattered, 16 * NT)
                    for t in range(NT):
                        pool.indirect_dma_start(
                            yg[:, t, :], None, sorted_y,
                            bass.IndirectOffsetOnAxis(ap=slot[:, t:t + 1], axis=0)).then_inc(gathered[t // C], 16)

        @block.scalar
        def _(act):
            a = nc.scalar
            act.dma_start(lams[:, 0, :], row(lq1).to_broadcast([P, HD])).then_inc(lam_dots, 16)
            act.dma_start(lams[:, 1, :], row(lq2).to_broadcast([P, HD])).then_inc(lam_dots, 16)
            act.dma_start(lams[:, 2, :], row(lk1).to_broadcast([P, HD])).then_inc(lam_dots, 16)
            act.dma_start(lams[:, 3, :], row(lk2).to_broadcast([P, HD])).then_inc(lam_dots, 16)
            act.wait_ge(lam_dots, 65)
            a.activation(lam_exp[:, :], lam_dot[:, :], ACT.Exp).then_inc(lam_exps, 1)
            for s in steps:
                kind = s[0]
                if kind == "norm":
                    b = s[1]
                    act.wait_ge(rstd_ready, b + 1)
                    for c in range(C):
                        last = a.activation(xn[:, C * b + c, :], xin[:, b % XB, c, :], ACT.Identity,
                                            bias=shift[:, b % 2, c:c + 1], scale=rstd[:, b % 2, c:c + 1])
                    last.then_inc(xn_ready, 1)
                elif kind == "project":
                    b, i = s[1:]
                    act.wait_ge(shared_filled, uses[s] + 1)
                    if b >= 1:
                        act.wait_ge(stacked[(b - 1) % STK], 12 * 16 * ((b - 1) // STK + 1))
                    a.activation(parts[:, i, 0, :], shared[:, :], ACT.Identity,
                                 bias=qk_bias[:, i:i + 1]).then_inc(high_ready, 1)
                elif kind == "exp":
                    n = s[1]
                    act.wait_ge(exp_filled, n + 1)
                    if n >= PR:
                        act.wait_ge(pv_done, (n - PR) // 4 + 1)
                    a.activation(probs[:, n % PR, :], exp_bank[n % 2][:, :], ACT.Exp,
                                 scale=SCALE).then_inc(exp_done, 1)
                elif kind == "copy_o":
                    grp = s[1]
                    act.wait_ge(pv_done, 4 * grp + 4)
                    if grp >= 2:
                        act.wait_ge(shared_filled, uses[("turn_o", grp - 2)] + 1)
                    a.activation(oT[:, grp % 2, :], pv_bank[:, :], ACT.Copy).then_inc(o_copied, 1)
                elif kind == "turn_z":
                    act.wait_ge(shared_filled, uses[s] + 1)
                    if s[1] >= 1:
                        act.wait_ge(s_ready, s[1])
                    a.activation(zT[:, :], shared[:, :], ACT.Copy).then_inc(zT_ready, 1)
                elif kind == "hidden" and s[2] == 0:
                    f = s[1]
                    act.wait_ge(hid_filled[0], f + 1)
                    if f >= 2:
                        act.wait_ge(shared_filled, uses[("down", f - 2)] + 1)
                    for c in range(FC):
                        last = a.activation(hT[:, f % 2, c, :], hid_bank[0][:, c * P:(c + 1) * P], ACT.Relu,
                                            bias=pair[:, f % WB, T_B1 + c:T_B1 + c + 1])
                    last.then_inc(hid_ready[0], 1)
                elif kind == "gate":
                    for half in range(2):
                        for b in range(B // 2 * half, B // 2 * (half + 1)):
                            act.wait_ge(gathered[b], 16 * C)
                        part = yg[:, NT // 2 * half:NT // 2 * (half + 1), :]
                        a.activation(part, part, ACT.Silu, scale=0.5).then_inc(gate_ready, 1)

        @block.vector
        def _(dve):
            v = nc.vector
            chain = [0]

            def link(ins):
                chain[0] += 1
                ins.then_inc(dve_chain, 1)
                dve.wait_ge(dve_chain, chain[0])

            for i in range(STK):
                v.memset(ks[MAX_ROW:KROWS, i, :, :], 1.0)
            v.memset(zeros, 0.0)
            link(v.memset(va[:, :, :, :, HD:VW], 0.0))
            v.memset(va[:, :, :, :, HD:HD + 1], 1.0).then_inc(dve_consts, 1)

            def fold():
                dve.wait_ge(lam_dots, 64)
                link(v.tensor_tensor(lam_prod[:, :, :], lams[:, 0:2, :], lams[:, 2:4, :], ALU.mult))
                v.tensor_reduce(lam_dot[:, :], lam_prod[:, :, :], AX.X, ALU.add).then_inc(lam_dots, 1)
                dve.wait_ge(lam_exps, 1)
                link(v.tensor_tensor(neg_lam[:, :], lam_exp[:, 1:2], lam_exp[:, 0:1], ALU.subtract))
                link(v.tensor_scalar(neg_lam[:, :], neg_lam[:, :], -LAM_INIT, None, ALU.add))
                dve.wait_ge(small_loaded, 16 * SMALL)
                for i, w in enumerate((wq_sb, wk_sb)):
                    v.tensor_copy(wqk[:, i, :].rearrange("p (d h) -> p h d", d=HD),
                                  w[:, :].rearrange("p (h d) -> p h d", d=HD))
                w = HALF * HD
                v.scalar_tensor_tensor(wv_eff[:, :], wv_sb[:, w:2 * w], neg_lam[:, 0:1], wv_sb[:, 0:w],
                                       ALU.mult, ALU.add)
                v.scalar_tensor_tensor(bv_eff[:, :], bv_sb[:, w:2 * w], neg_lam[:, 0:1], bv_sb[:, 0:w],
                                       ALU.mult, ALU.add)
                link(v.tensor_scalar(wo_eff[:, :], wo_sb[:, :], lnw_sb[:, 0:1], OUT_SCALE, ALU.mult, ALU.mult))
                dve.wait_ge(consts_ready, 1)
                v.tensor_scalar(lnb_wide[:, :], ones[:, :], lnb_sb[:, 0:1], OUT_SCALE,
                                ALU.mult, ALU.mult).then_inc(folded, 1)
                dve.wait_ge(shared_filled, 1)
                link(v.tensor_tensor(bo_eff[:, :], shared[:, 0:D], bo_sb[:, :], ALU.add))
                v.memset(v01[:, 0:1], 0.0).then_inc(shared_free, 1)

            def build_table():
                dve.wait_ge(expert_loaded, 16 * (4 + 2 * (EXP + 1)))
                tab = table[:, :].rearrange("p (e w) -> p e w", e=EXP + 1)
                b2v = b2_sb
                v.tensor_copy(tab[:, EXP, T_B2:T_B2 + D], b2v[:, EXP, :])
                v.tensor_tensor(tab[:, 0:EXP, T_B2:T_B2 + D], b2v[:, 0:EXP, :], b2v[:, 1:EXP + 1, :],
                                ALU.add).then_inc(table_ready, 1)

            def route(use):
                dve.wait_ge(xn_ready, B)
                dve.wait_ge(iota_ready, 1)
                link(v.tensor_tensor(v01[:, :], xn[:, :, 0], xn[:, :, 1], ALU.add))
                link(v.scalar_tensor_tensor(v_abs[:, :], v01[:, :], -1.0, v01[:, :], ALU.mult, ALU.max))
                c3 = cmp[:, 0:NT * 15].rearrange("p (t k) -> p t k", k=15)
                link(v.tensor_tensor(c3, v_abs[:, :].unsqueeze(2).to_broadcast([P, NT, 15]),
                                     iota[:, 1:16].unsqueeze(1).to_broadcast([P, NT, 15]), ALU.is_ge))
                link(v.tensor_reduce(n_abs[:, :], c3, AX.X, ALU.add))
                link(v.tensor_scalar(sign[:, :], v01[:, :], 0.0, 2.0, ALU.is_ge, ALU.mult))
                link(v.scalar_tensor_tensor(h[:, :], sign[:, :], -1.0, n_abs[:, :], ALU.add, ALU.mult))
                v.tensor_scalar(wrap[:, 0, :], h[:, :], 0.0, 8.0, ALU.is_lt, ALU.mult)
                v.tensor_scalar(wrap[:, 1, :], h[:, :], -8.0, 8.0, ALU.is_lt, ALU.mult)
                link(v.tensor_scalar(wrap[:, 2, :], h[:, :], 8.0, -8.0, ALU.is_ge, ALU.mult))
                for i in range(3):
                    link(v.tensor_tensor(h[:, :], h[:, :], wrap[:, i, :], ALU.add))
                link(v.tensor_tensor(onehot[:, :, :], h[:, :].unsqueeze(1).to_broadcast([P, EXP, NT]),
                                     iota[:, 0:EXP].unsqueeze(2).to_broadcast([P, EXP, NT]), ALU.is_equal))
                v.tensor_reduce(count[:, :], onehot[:, :, :], AX.X, ALU.add).then_inc(count_ready, 1)
                flat = work[:, 768:1024]
                link(v.tensor_tensor_scan(flat, work[:, 512:768], zeros,
                                          0.0, ALU.add, ALU.add))
                link(v.tensor_tensor(seen[:, :, :], seen[:, :, :], onehot[:, :, :], ALU.subtract))
                dve.wait_ge(shared_filled, use + 1)
                c2 = cmp[:, 0:EXP * NT].rearrange("p (e k) -> p e k", k=NT)
                link(v.tensor_scalar(tile_base[:, :], shared[:, EXP:2 * EXP], 1.0 / P, None, ALU.mult))
                link(v.tensor_tensor(c2, tile_base[:, :].unsqueeze(2).to_broadcast([P, EXP, NT]),
                                     iota[:, 0:NT].unsqueeze(1).to_broadcast([P, EXP, NT]), ALU.is_gt))
                link(v.tensor_reduce(tiles_of[:, :], c2, AX.X, ALU.add))
                link(v.tensor_tensor_scan(tile_end[:, :], tiles_of[:, :], zeros[:, 0:EXP], 0.0, ALU.add, ALU.add))
                link(v.tensor_tensor(tile_base[:, :], tile_end[:, :], tiles_of[:, :], ALU.subtract))
                link(v.scalar_tensor_tensor(base[:, :], tile_base[:, :], float(P), shared[:, 0:EXP],
                                            ALU.mult, ALU.add))
                link(v.tensor_tensor(base[:, :], base[:, :], seen[:, :, 0], ALU.subtract))
                link(v.tensor_tensor(seen[:, :, :], seen[:, :, :],
                                     base[:, :].unsqueeze(2).to_broadcast([P, EXP, NT]), ALU.add))
                link(v.tensor_tensor(seen[:, :, :], seen[:, :, :], onehot[:, :, :], ALU.mult))
                link(v.tensor_reduce(slot_f[:, :], seen[:, :, :].rearrange("p e t -> p t e"), AX.X, ALU.add))
                v.tensor_copy(slot[:, :], slot_f[:, :]).then_inc(slots_ready, 1)
                c1 = cmp[:, 0:FT * (EXP - 1)].rearrange("p (f e) -> p f e", e=EXP - 1)
                link(v.tensor_tensor(c1, iota[:, 0:FT].unsqueeze(2).to_broadcast([P, FT, EXP - 1]),
                                     tile_base[:, 1:EXP].unsqueeze(1).to_broadcast([P, FT, EXP - 1]), ALU.is_ge))
                link(v.tensor_reduce(texp_f[:, :], c1, AX.X, ALU.add))
                v.tensor_copy(texp[:, :], texp_f[:, :]).then_inc(texp_ready, 1)
                v.memset(v01[:, 0:1], 0.0).then_inc(shared_free, 1)

            for s in steps:
                kind = s[0]
                if kind == "norm":
                    b = s[1]
                    dve.wait_ge(x_loaded[b], 16)
                    if b >= 1:
                        dve.wait_ge(stats_ready, b)
                    if b >= 2:
                        dve.wait_ge(rstd_ready, b - 1)
                    for c in range(C):
                        last = v.bn_stats(stats[:, c, :], xin[:, b % XB, c, :])
                    link(last)
                    for c in range(C):
                        last = v.bn_aggr(mv[:, b % 2, c, :], stats[:, c, :])
                    last.then_inc(stats_ready, 1)
                    if b == 0:
                        fold()
                elif kind == "transpose_x":
                    b = s[1]
                    dve.wait_ge(shared_filled, uses[s] + 1)
                    if b >= 2:
                        dve.wait_ge(shared_filled, uses[("values", b - 2)] + 1)
                    v.tensor_copy(xT[:, b % 2, :], shared[:, :]).then_inc(xT_ready, 1)
                elif kind == "project":
                    b, i = s[1:]
                    dve.wait_ge(high_ready, 2 * b + i + 1)
                    if b + i >= 1:
                        dve.wait_ge(low_ready, 2 * b + i)
                    v.scalar_tensor_tensor(rest[:, :], shared[:, :], qk_bias[:, i:i + 1], parts[:, i, 0, :],
                                           ALU.add, ALU.subtract).then_inc(rest_ready, 1)
                elif kind == "values":
                    b = s[1]
                    dve.wait_ge(shared_filled, uses[s] + 1)
                    if b >= 2:
                        dve.wait_ge(pv_done, 8 * (b - 1))
                    w = HALF * HD
                    v.tensor_tensor(va[:, b % 2, :, :, 0:HD],
                                    shared[:, 0:C * w].rearrange("p (c i d) -> p c i d", c=C, d=HD),
                                    bv_eff[:, :].rearrange("p (i d) -> p i d", d=HD).unsqueeze(1)
                                    .to_broadcast([P, C, HALF, HD]), ALU.add).then_inc(va_ready, 1)
                elif kind == "score":
                    n = s[1]
                    b, col = divmod(n, HEADS * C)
                    dve.wait_ge(score_filled, n + 1)
                    if col == 0 and b >= 2:
                        dve.wait_ge(max_split, b - 1)
                    v.tensor_reduce(neg_max[:, b % 2, col:col + 1], score_bank[n % 2][:, :], AX.X, ALU.max,
                                    negate=True).then_inc(max_taken, 1)
                elif kind == "row_max":
                    b = s[1]
                    dve.wait_ge(shared_filled, uses[s] + 1)
                    if b >= 1:
                        dve.wait_ge(max_stacked, 16 * PARTS * b)
                    rows = shared[0:HEADS * C, 0:P]
                    link(v.tensor_copy(max_parts[:, 0, :], rows))
                    link(v.tensor_tensor(max_rest[:, :], rows, max_parts[:, 0, :], ALU.subtract))
                    link(v.tensor_copy(max_parts[:, 1, :], max_rest[:, :]))
                    v.tensor_tensor(max_parts[:, 2, :], max_rest[:, :], max_parts[:, 1, :],
                                    ALU.subtract).then_inc(max_split, 1)
                elif kind == "turn_o":
                    grp = s[1]
                    b, g2 = divmod(grp, 2)
                    dve.wait_ge(shared_filled, uses[s] + 1)
                    if grp >= 4:
                        dve.wait_ge(z_ready, b - 1)
                    o4 = shared[:, :].rearrange("p (c i w) -> p c i w", c=C, w=VW)
                    link(v.reciprocal(inv_sum[:, :], shared[:, :].rearrange("p (n w) -> p n w", w=VW)[:, :, HD]))
                    v.tensor_tensor(attn[:, b % 2, :, g2 * HALF * HD:(g2 + 1) * HALF * HD]
                                    .rearrange("p c (i d) -> p c i d", d=HD), o4[:, :, :, 0:HD],
                                    inv_sum[:, :].rearrange("p (c i) -> p c i", c=C).unsqueeze(3)
                                    .to_broadcast([P, C, HALF, HD]), ALU.mult).then_inc(attn_ready, 1)
                elif kind == "norm_o":
                    b = s[1]
                    dve.wait_ge(attn_ready, 2 * b + 2)
                    if b >= 1:
                        dve.wait_ge(z_ready, b)
                    for c in range(C):
                        last = v.bn_stats(stats_o[:, c, :], attn[:, b % 2, c, :])
                    link(last)
                    for c in range(C):
                        last = v.bn_aggr(mv_o[:, c, :], stats_o[:, c, :])
                    last.then_inc(stats_o_ready, 1)
                elif kind == "project_o":
                    b = s[1]
                    dve.wait_ge(shared_filled, uses[s] + 1)
                    v.tensor_tensor(s_sb[:, C * b:C * b + C, :], shared[:, :].rearrange("p (c n) -> p c n", c=C),
                                    bo_eff[:, :].unsqueeze(1).to_broadcast([P, C, D]), ALU.add).then_inc(s_ready, 1)
                elif kind == "route":
                    build_table()
                    route(uses[s])
                elif kind == "turn_tile":
                    f = s[1]
                    dve.wait_ge(shared_filled, uses[s] + 1)
                    if f >= 2:
                        dve.wait_ge(hid_filled[1], f - 1)
                    v.tensor_copy(xsT[:, f % 2, :], shared[:, 0:P]).then_inc(xsT_ready, 1)
                elif kind == "hidden" and s[2] == 1:
                    f = s[1]
                    dve.wait_ge(hid_filled[1], f + 1)
                    if f >= 2:
                        dve.wait_ge(shared_filled, uses[("down", f - 2)] + 1)
                    for c in range(FC):
                        last = v.tensor_scalar(hT[:, f % 2, FC + c, :], hid_bank[1][:, c * P:(c + 1) * P],
                                               pair[:, f % WB, TW + T_B1 + c:TW + T_B1 + c + 1], 0.0,
                                               ALU.add, ALU.max)
                    last.then_inc(hid_ready[1], 1)
                elif kind == "down":
                    f = s[1]
                    dve.wait_ge(shared_filled, uses[s] + 1)
                    if f >= 2:
                        dve.wait_ge(y_stored[f % 2], 16 * (f // 2))
                    v.tensor_tensor(y_sb[:, f % 2, :], shared[:, 0:D], pair[:, f % WB, T_B2:T_B2 + D],
                                    ALU.add).then_inc(y_ready, 1)
                elif kind == "finish":
                    b = s[1]
                    dve.wait_ge(gate_ready, 1 if b < B // 2 else 2)
                    dve.wait_ge(x_reloaded[b], 16)
                    dve.wait_ge(s_ready, b + 1)
                    tok = slice(C * b, C * b + C)
                    link(v.tensor_tensor(s_sb[:, tok, :], s_sb[:, tok, :], yg[:, tok, :], ALU.mult))
                    v.tensor_tensor(s_sb[:, tok, :], s_sb[:, tok, :], x_again[:, b % 2, :, :],
                                    ALU.add).then_inc(out_ready, 1)

        @block.tensor
        def _(pe):
            t = nc.tensor

            def free(use):
                pe.wait_ge(shared_free_of(use - 1)[0], shared_free_of(use - 1)[1])

            reader = {0: (shared_free, 1)}
            for s, use in uses.items():
                kind = s[0]
                reader[use] = {
                    "transpose_x": lambda: (xT_ready, s[1] + 1),
                    "project": lambda: (rest_ready, 2 * s[1] + s[2] + 1),
                    "values": lambda: (va_ready, s[1] + 1),
                    "row_max": lambda: (max_split, s[1] + 1),
                    "turn_o": lambda: (attn_ready, s[1] + 1),
                    "turn_z": lambda: (zT_ready, s[1] + 1),
                    "project_o": lambda: (s_ready, s[1] + 1),
                    "route": lambda: (shared_free, 2),
                    "turn_tile": lambda: (xsT_ready, s[1] + 1),
                    "down": lambda: (y_ready, s[1] + 1),
                }[kind]()

            def shared_free_of(use):
                return reader[use]

            pe.wait_ge(folded, 1)
            pe.wait_ge(consts_ready, 1)
            t.matmul(shared[:, 0:D], lnb_wide[:, :], wo_sb[:, :], start=True, stop=True).then_inc(shared_filled, 1)
            expert = [None] * FT
            for s in steps:
                kind = s[0]
                if kind == "transpose_x":
                    b = s[1]
                    pe.wait_ge(xn_ready, b + 1)
                    free(uses[s])
                    for c in range(C):
                        last = t.transpose(shared[:, c * P:(c + 1) * P], xn[:, C * b + c, :], ident[:, :])
                    last.then_inc(shared_filled, 1)
                elif kind == "project":
                    b, i = s[1:]
                    if i == 0:
                        pe.wait_ge(xT_ready, b + 1)
                    free(uses[s])
                    t.matmul(shared[:, :], wqk[:, i, :], xT[:, b % 2, :], start=True, stop=True).then_inc(shared_filled, 1)
                elif kind == "values":
                    b = s[1]
                    free(uses[s])
                    w = HALF * HD
                    for c in range(C):
                        last = t.matmul(shared[:, c * w:(c + 1) * w], xT[:, b % 2, c * P:(c + 1) * P], wv_eff[:, :],
                                        start=True, stop=True)
                    last.then_inc(shared_filled, 1)
                elif kind == "score":
                    n = s[1]
                    b, col = divmod(n, HEADS * C)
                    hh, c = divmod(col, C)
                    if col == 0:
                        pe.wait_ge(stacked[b % STK], 12 * 16 * (b // STK + 1))
                    if n >= 2:
                        pe.wait_ge(max_taken, n - 1)
                    t.matmul(score_bank[n % 2][:, :], qs[0:MAX_ROW, b % STK, hh, c * P:(c + 1) * P],
                             ks[0:MAX_ROW, b % STK, hh, :], start=True, stop=True).then_inc(score_filled, 1)
                elif kind == "row_max":
                    b = s[1]
                    pe.wait_ge(max_taken, HEADS * C * (b + 1))
                    free(uses[s])
                    t.transpose(shared[0:HEADS * C, 0:P], neg_max[:, b % 2, :], ident[:, :]).then_inc(shared_filled, 1)
                elif kind == "exp":
                    n = s[1]
                    b, r = divmod(n, HEADS * C)
                    g2, r = divmod(r, C * HALF)
                    kc, i = divmod(r, HALF)
                    hh = g2 * HALF + i
                    if n % (HEADS * C) == 0:
                        pe.wait_ge(max_stacked, 16 * PARTS * (b + 1))
                        if b == 0:
                            pe.wait_ge(dve_consts, 1)
                    if n >= 2:
                        pe.wait_ge(exp_done, n - 1)
                    t.matmul(exp_bank[n % 2][:, :], ks[0:KROWS, b % STK, hh, kc * P:(kc + 1) * P],
                             qs[0:KROWS, b % STK, hh, :], start=True, stop=True).then_inc(exp_filled, 1)
                elif kind == "pv":
                    n4 = s[1]
                    grp, kc = divmod(n4, C)
                    b = grp // 2
                    pe.wait_ge(exp_done, 4 * n4 + 4)
                    if n4 % (2 * C) == 0:
                        pe.wait_ge(va_ready, b + 1)
                    if kc == 0 and grp >= 1:
                        pe.wait_ge(o_copied, grp)
                    for i in range(HALF):
                        last = t.matmul(pv_bank[VW * i:VW * (i + 1), :], va[:, b % 2, kc, i, :],
                                        probs[:, (4 * n4 + i) % PR, :], start=(kc == 0), stop=(kc == C - 1))
                    last.then_inc(pv_done, 1)
                elif kind == "turn_o":
                    grp = s[1]
                    pe.wait_ge(o_copied, grp + 1)
                    free(uses[s])
                    for c in range(C):
                        last = t.transpose(shared[:, c * P:(c + 1) * P], oT[:, grp % 2, c * P:(c + 1) * P], ident[:, :])
                    last.then_inc(shared_filled, 1)
                elif kind == "turn_z":
                    pe.wait_ge(z_ready, s[1] + 1)
                    free(uses[s])
                    for c in range(C):
                        last = t.transpose(shared[:, c * P:(c + 1) * P], z[:, c, :], ident[:, :])
                    last.then_inc(shared_filled, 1)
                elif kind == "project_o":
                    pe.wait_ge(zT_ready, s[1] + 1)
                    free(uses[s])
                    for c in range(C):
                        last = t.matmul(shared[:, c * D:(c + 1) * D], zT[:, c * P:(c + 1) * P], wo_eff[:, :],
                                        start=True, stop=True)
                    last.then_inc(shared_filled, 1)
                elif kind == "route":
                    pe.wait_ge(count_ready, 1)
                    free(uses[s])
                    t.matmul(shared[:, 0:EXP], before[:, :], count[:, :], start=True, stop=True)
                    t.matmul(shared[:, EXP:2 * EXP], ones[:, :], count[:, :], start=True, stop=True).then_inc(shared_filled, 1)
                elif kind == "turn_tile":
                    f = s[1]
                    pe.wait_ge(tile_loaded[f % 2], 16 * (f // 2 + 1))
                    free(uses[s])
                    t.transpose(shared[:, 0:P], xs[:, f % 2, :], ident[:, :]).then_inc(shared_filled, 1)
                elif kind == "hidden":
                    f, j = s[1:]
                    if j == 0:
                        pe.wait_ge(pair_loaded[f % WB], 16 * (f // WB + 1))
                        pe.wait_ge(xsT_ready, f + 1)
                    if f >= 1:
                        pe.wait_ge(hid_ready[j], f)
                    for c in range(FC):
                        o = j * TW + T_W1 + c * P
                        last = t.matmul(hid_bank[j][:, c * P:(c + 1) * P], pair[:, f % WB, o:o + P], xsT[:, f % 2, :],
                                        start=True, stop=True)
                    last.then_inc(hid_filled[j], 1)
                elif kind == "down":
                    f = s[1]
                    pe.wait_ge(hid_ready[0], f + 1)
                    pe.wait_ge(hid_ready[1], f + 1)
                    free(uses[s])
                    e = pe.value_load(texp[0:1, f:f + 1], min_val=0, max_val=EXP - 1)
                    for k in range(2 * FC):
                        last = t.matmul(shared[:, 0:D], hT[:, f % 2, k, :], w2_sb[:, bass.ds(e * FF + k * D, D)],
                                        start=(k == 0), stop=(k == 2 * FC - 1))
                    last.then_inc(shared_filled, 1)


_INS = ["L0_attn_hidden_states", "L0_attn_Wq", "L0_attn_bq", "L0_attn_Wk", "L0_attn_bk", "L0_attn_Wv", "L0_attn_bv",
        "L0_attn_Wo", "L0_attn_bo", "L0_attn_lambda_q1", "L0_attn_lambda_k1", "L0_attn_lambda_q2",
        "L0_attn_lambda_k2", "L0_attn_ln_w", "L0_attn_ln_b", "L0_ffn_W1", "L0_ffn_b1", "L0_ffn_W2", "L0_ffn_b2"]
_OUTS = [((8, 512, 128), "float32")]


def kernel(**inputs):
    import numpy as _np
    import concourse.bacc as _bacc
    from concourse import mybir as _mybir
    from concourse.bass_utils import run_bass_kernel_spmd as _run

    nc = _bacc.Bacc("TRN2", target_bir_lowering=False, num_devices=1)
    arrays, args = {}, []
    for name in _INS:
        a = _np.ascontiguousarray(inputs[name])
        arrays[f"in_{name}_dram"] = a
        args.append(nc.dram_tensor(f"in_{name}_dram", a.shape, _mybir.dt.from_np(a.dtype), kind="ExternalInput").ap())
    for i, (shape, dtype) in enumerate(_OUTS):
        dt = _mybir.dt.from_np(_np.dtype(dtype))
        args.append(nc.dram_tensor(f"out_{i}_dram", shape, dt, kind="ExternalOutput").ap())
    gated_attention_moe(nc, *args)
    r = _run(nc, [arrays], core_ids=[0])
    return r.results[0]["out_0_dram"]
```

```python
import concourse.bass as bass
from concourse import mybir
from contextlib import ExitStack

F32 = mybir.dt.float32
BF16 = mybir.dt.bfloat16
I32 = mybir.dt.int32
ALU = mybir.AluOpType
ACT = mybir.ActivationFunctionType
AX = mybir.AxisListType

P = 128
B, S, D = 8, 512, 128
HEADS, HD = 8, 16
HALF = HEADS // 2
C = S // P
NT = B * C
EXP = 8
FF = 4 * D
FC = FF // P
FT = NT + (EXP * (P - 1)) // P
LAM_INIT = 0.8
OUT_SCALE = 1.0 - LAM_INIT
EPS = 1e-5
SCALE = 1.0 / HD ** 0.5
PARTS = 3
Q_PART = [0, 1, 2, 0, 1, 0]
K_PART = [0, 0, 0, 1, 1, 2]
MAX_ROW = len(Q_PART) * HD
KROWS = MAX_ROW + PARTS
VW = 32
STK = 3
PR = 8
T_B2, T_W1, T_B1 = 0, D, D + FF
TW = D + FF + FC
LAG = 24
FFN_FIRST, FFN_PACE = 60.0, 4.35
RING = 3
WB = 3


def schedule():
    steps = []

    def at(time, *step):
        steps.append((time, len(steps), step))

    for b in range(B):
        at((-30, -29.8, -29.6, -29.4, -25.5, -24.5, -23.6, -23.2)[b], "norm", b)
        qkv = -27 if b == 0 else 32 * b - 24
        at(qkv, "transpose_x", b)
        at(qkv + 3 if b else -26, "project", b, 0)
        at(qkv + 7 if b else -25, "project", b, 1)
        at(32 * b + LAG - 27.8 if b else -24, "values", b)
        for j in range(4):
            at(qkv + (9.5, 11, 14, 15.5)[j] if b else -23 + 0.1 * j, "stack", b, j)
        for n in range(32 * b, 32 * b + 32):
            at(n, "score", n)
            at(n + LAG, "exp", n)
            if n % 4 == 3:
                at(n + LAG + 3.5, "pv", n // 4)
        for grp in (2 * b, 2 * b + 1):
            at(16 * grp + 15.5, "split_max", grp)
            at(16 * grp + 18.5, "turn_max", grp)
            at(16 * grp + LAG + 20, "copy_o", grp)
            at(16 * grp + LAG + 22.2, "turn_o", grp)
        at(32 * b + LAG + 39.5, "norm_o", b)
        at(32 * b + LAG + 43.8, "scale_o", b)
        at(32 * b + LAG + 46.3, "turn_z", b)
        at(32 * b + LAG + 49.3, "project_o", b)
    at(-28, "fold")
    at(30.3, "b1")
    at(31.3, "table")
    at(-12, "route")
    at(-11, "scatter")
    f0, pace = FFN_FIRST, FFN_PACE
    for f in range(FT):
        t = f0 + pace * f
        at(t - 1.5 * pace, "load_tile", f)
        at(t - 0.25 * pace, "turn_tile", f)
        at(t, "hidden", f, 0)
        at(t + 0.45 * pace, "hidden", f, 1)
        at(t + 1.15 * pace, "down", f)
        at(t + 1.3 * pace, "store_tile", f)
    end = f0 + pace * (FT + 0.5)
    for b in range(B):
        at(end + 3.9 * b, "gather", b)
    gate = 32 * B + LAG + 4.5
    at(gate, "gate")
    for b in range(B):
        at(max(32 * b + LAG + 55, gate + 1 + b), "finish", b)
    return [s for _, _, s in sorted(steps)]


def gated_attention_moe(nc, x, wq, bq, wk, bk, wv, bv, wo, bo, lq1, lk1, lq2, lk2,
                        ln_w, ln_b, w1, b1, w2, b2, out):
    steps = schedule()
    uses = {}
    for s in steps:
        if s[0] in ("transpose_x", "project", "values", "turn_max", "turn_o", "turn_z", "project_o",
                    "route", "b1", "turn_tile", "down", "hidden"):
            uses[s] = len(uses) + 1

    x_v = x.rearrange("b (c p) d -> b p c d", p=P)
    out_v = out.rearrange("b (c p) d -> b p c d", p=P)
    sorted_x = nc.dram_tensor("sorted_x", (FT * P, D), F32, kind="Internal").ap()
    sorted_y = nc.dram_tensor("sorted_y", (FT * P, D), F32, kind="Internal").ap()

    ctx = ExitStack()
    with ctx:
        def sb(name, shape, dt=F32):
            return ctx.enter_context(nc.sbuf_tensor(name, shape, dt))

        def bank(name):
            return ctx.enter_context(nc.psum_tensor(name, [P, 512], F32))

        def sem(name):
            return ctx.enter_context(nc.semaphore(name))

        ident = sb("ident", [P, P])
        before = sb("before", [P, P])
        ones = sb("ones", [P, P])
        iota_i = sb("iota_i", [P, 40], I32)
        iota = sb("iota", [P, 40])
        neg_half = sb("neg_half", [P, C])
        wq_sb = sb("wq_sb", [P, D])
        wk_sb = sb("wk_sb", [P, D])
        wv_sb = sb("wv_sb", [P, D])
        wo_sb = sb("wo_sb", [P, D])
        wqk = sb("wqk", [P, 2, D])
        qk_bias = sb("qk_bias", [P, 2])
        bv_sb = sb("bv_sb", [P, D])
        bo_sb = sb("bo_sb", [P, D])
        lams = sb("lams", [P, 4, HD])
        lam_prod = sb("lam_prod", [P, 2, HD])
        lam_dot = sb("lam_dot", [P, 2])
        lam_exp = sb("lam_exp", [P, 2])
        neg_lam = sb("neg_lam", [P, 1])
        lnw_sb = sb("lnw_sb", [P, 1])
        lnb_sb = sb("lnb_sb", [P, 1])
        lnb_wide = sb("lnb_wide", [P, P])
        wv_eff = sb("wv_eff", [P, HALF * HD])
        bv_eff = sb("bv_eff", [P, HALF * HD])
        wo_eff = sb("wo_eff", [P, D])
        bo_eff = sb("bo_eff", [P, D])
        table = sb("table", [P, (EXP + 1) * TW])
        w2_sb = sb("w2_sb", [P, (EXP + 1) * FF])
        xn = sb("xn", [P, NT, D])
        yg = xn
        stats = sb("stats", [P, C, 6])
        mv = sb("mv", [P, 2, C, 2])
        var_eps = sb("var_eps", [P, C])
        rstd = sb("rstd", [P, 2, C])
        shift = sb("shift", [P, 2, C])
        xT = sb("xT", [P, 2, S])
        parts = sb("parts", [P, 2, PARTS, S], BF16)
        rest = sb("rest", [P, 2, S])
        qs = sb("qs", [P, STK, HEADS, S], BF16)
        ks = sb("ks", [P, STK, HEADS, S], BF16)
        va = sb("va", [P, 2, C, HALF, VW])
        neg_max = sb("neg_max", [P, 2, HEADS * C])
        max_parts = sb("max_parts", [P, 2, PARTS, 16], BF16)
        max_rest = sb("max_rest", [P, 2, 16])
        max_rows = sb("max_rows", [PARTS * 16, 2, P], BF16)
        ident_bf = sb("ident_bf", [P, P], BF16)
        ones_bf = sb("ones_bf", [PARTS, S], BF16)
        b1_rows = sb("b1_rows", [EXP * FC, P])
        probs = sb("probs", [P, PR, S])
        oT = sb("oT", [P, 2, S])
        inv_sum = sb("inv_sum", [P, C * HALF])
        attn = sb("attn", [P, 2, C, D])
        stats_o = sb("stats_o", [P, C, 6])
        mv_o = sb("mv_o", [P, C, 2])
        var_eps_o = sb("var_eps_o", [P, C])
        rstd_o = sb("rstd_o", [P, C])
        shift_o = sb("shift_o", [P, C])
        z = sb("z", [P, C, D])
        zT = sb("zT", [P, S])
        s_sb = sb("s_sb", [P, NT, D])
        xin = s_sb
        v01 = sb("v01", [P, NT])
        v_abs = sb("v_abs", [P, NT])
        n_abs = sb("n_abs", [P, NT])
        sign = sb("sign", [P, NT])
        h = sb("h", [P, NT])
        wrap = sb("wrap", [P, 3, NT])
        count = sb("count", [P, EXP])
        tiles_of = sb("tiles_of", [P, EXP])
        tile_end = sb("tile_end", [P, EXP])
        tile_base = sb("tile_base", [P, EXP])
        base = sb("base", [P, EXP])
        slot_f = sb("slot_f", [P, NT])
        slot = sb("slot", [P, NT], I32)
        texp_f = sb("texp_f", [P, FT])
        texp = sb("texp", [P, FT], I32)
        xs = sb("xs", [P, 2, D])
        xsT = sb("xsT", [P, 2, P])
        pair = sb("pair", [P, WB, 2 * TW])
        x_again = pair[:, :, :].rearrange("p a n -> p (a n)")[:, 0:2 * C * D].rearrange("p (a c d) -> p a c d", a=2, c=C)
        hT = sb("hT", [P, 2, 2 * FC, P])
        work = hT[:, :, :, :].rearrange("p a k n -> p (a k n)")
        cmp = work[:, 0:512]
        onehot = work[:, 512:768].rearrange("p (e t) -> p e t", e=EXP)
        seen = work[:, 768:1024].rearrange("p (e t) -> p e t", e=EXP)
        zeros = work[:, 1024:1024 + EXP * NT]
        y_sb = sb("y_sb", [P, 2, D])

        score_bank = [bank("score0"), bank("score1")]
        exp_bank = [bank("exp0"), bank("exp1")]
        pv_bank = bank("pv_bank")
        ring = [bank(f"ring{i}") for i in range(RING)]

        consts_ready = sem("consts_ready")
        iota_ready = sem("iota_ready")
        dve_consts = sem("dve_consts")
        small_loaded = sem("small_loaded")
        expert_loaded = sem("expert_loaded")
        b1_loaded = sem("b1_loaded")
        lam_dots = sem("lam_dots")
        lam_exps = sem("lam_exps")
        folded = sem("folded")
        lnb_ready = sem("lnb_ready")
        table_ready = sem("table_ready")
        x_loaded = [sem(f"x_loaded{b}") for b in range(B)]
        x_reloaded = [sem(f"x_reloaded{b}") for b in range(B)]
        stats_ready = sem("stats_ready")
        rstd_ready = sem("rstd_ready")
        xn_ready = sem("xn_ready")
        shared_filled = sem("shared_filled")
        shared_free = sem("shared_free")
        xT_ready = sem("xT_ready")
        high_ready = sem("high_ready")
        rest_ready = sem("rest_ready")
        mid_ready = sem("mid_ready")
        low_ready = sem("low_ready")
        stacked = [sem(f"stacked{i}") for i in range(STK)]
        parts_sent = sem("parts_sent")
        va_ready = sem("va_ready")
        score_filled = sem("score_filled")
        max_taken = sem("max_taken")
        max_split = sem("max_split")
        max_turned = sem("max_turned")
        max_stacked = sem("max_stacked")
        b1_ready = sem("b1_ready")
        ones_stacked = sem("ones_stacked")
        exp_filled = sem("exp_filled")
        exp_done = sem("exp_done")
        pv_done = sem("pv_done")
        o_copied = sem("o_copied")
        attn_ready = sem("attn_ready")
        stats_o_ready = sem("stats_o_ready")
        rstd_o_ready = sem("rstd_o_ready")
        z_ready = sem("z_ready")
        zT_ready = sem("zT_ready")
        s_ready = sem("s_ready")
        sorted_zeroed = sem("sorted_zeroed")
        slots_ready = sem("slots_ready")
        count_ready = sem("count_ready")
        texp_ready = sem("texp_ready")
        scattered = sem("scattered")
        tile_loaded = [sem(f"tile_loaded{i}") for i in range(2)]
        pair_loaded = [sem(f"pair_loaded{i}") for i in range(WB)]
        xsT_ready = sem("xsT_ready")
        hid_ready = [sem(f"hid_ready{j}") for j in range(2)]
        y_ready = sem("y_ready")
        y_stored = [sem(f"y_stored{i}") for i in range(2)]
        gathered = [sem(f"gathered{b}") for b in range(B)]
        gate_ready = sem("gate_ready")
        out_ready = sem("out_ready")
        out_stored = sem("out_stored")
        dve_chain = sem("dve_chain")
        pool_chain = sem("pool_chain")
        act_chain = sem("act_chain")

        block = ctx.enter_context(nc.Block())

        def row(ap):
            return ap.rearrange("(a n) -> a n", a=1)

        SMALL = 10

        @block.sync
        def _(sp):
            def load_x(b):
                sp.dma_start(xin[:, C * b:C * b + C, :], x_v[b]).then_inc(x_loaded[b], 16)

            load_x(0)
            load_x(1)
            sp.dma_start(wq_sb[:, :], wq).then_inc(small_loaded, 16)
            sp.dma_start(wk_sb[:, :], wk).then_inc(small_loaded, 16)
            sp.dma_start(wv_sb[:, :], wv).then_inc(small_loaded, 16)
            sp.dma_start(wo_sb[:, :], wo).then_inc(small_loaded, 16)
            sp.dma_start(bv_sb[:, :], row(bv).to_broadcast([P, D])).then_inc(small_loaded, 16)
            sp.dma_start(bo_sb[:, :], row(bo).to_broadcast([P, D])).then_inc(small_loaded, 16)
            for i, v in enumerate((bq, bk)):
                if True:
                    sp.dma_start(qk_bias[:, i:i + 1], v.rearrange("(h d) -> d h", d=HD),
                                 allow_slow_non_contiguous=True).then_inc(small_loaded, 16)
            sp.dma_start(lnw_sb[:, :], ln_w.rearrange("(p a) -> p a", a=1)).then_inc(small_loaded, 16)
            sp.dma_start(lnb_sb[:, :], ln_b.rearrange("(p a) -> p a", a=1)).then_inc(small_loaded, 16)
            for b in range(2, B):
                load_x(b)
            sp.wait_ge(dve_consts, 1)
            sp.dma_start(sorted_x.rearrange("(f p) d -> p f d", p=P),
                         zeros[:, 0:D].unsqueeze(1).to_broadcast([P, FT, D])).then_inc(sorted_zeroed, 16)
            for i in range(STK):
                sp.dma_start(ks[MAX_ROW:KROWS, i, :, :],
                             ones_bf[:, :].unsqueeze(1).to_broadcast([PARTS, HEADS, S])).then_inc(ones_stacked, 16)

            for s in steps:
                kind = s[0]
                if kind == "stack":
                    b, j = s[1:]
                    i, half = divmod(j, 2)
                    sp.wait_ge(low_ready, 2 * b + i + 1)
                    if b >= STK:
                        sp.wait_ge(exp_done, 32 * (b - STK + 1))
                    dst, order = ((qs, Q_PART), (ks, K_PART))[i]
                    for blk in range(3 * half, 3 * half + 3):
                        sp.dma_start(dst[blk * HD:(blk + 1) * HD, b % STK, :, :],
                                     parts[:, i, order[blk], :]).then_inc(stacked[b % STK], 16)
                elif kind == "turn_max":
                    grp = s[1]
                    b, g2 = divmod(grp, 2)
                    sp.wait_ge(max_turned, grp + 1)
                    sp.dma_start(qs[MAX_ROW:KROWS, b % STK, g2 * HALF:(g2 + 1) * HALF, :],
                                 max_rows[:, g2, :]).then_inc(max_stacked, 16)
                elif kind == "load_tile":
                    f = s[1]
                    if f == 0:
                        sp.wait_ge(scattered, 16 * NT)
                        sp.wait_ge(texp_ready, 1)
                        sp.wait_ge(table_ready, 1)
                        sp.wait_ge(b1_ready, 1)
                    if f >= 2:
                        sp.wait_ge(xsT_ready, f - 1)
                    sp.dma_start(xs[:, f % 2, :], sorted_x[f * P:(f + 1) * P, :]).then_inc(tile_loaded[f % 2], 16)
                    if f >= WB:
                        sp.wait_ge(y_ready, f - WB + 1)
                    e = sp.value_load(texp[0:1, f:f + 1], min_val=0, max_val=EXP - 1)
                    sp.dma_start(pair[:, f % WB, :], table[:, bass.ds(e * TW, 2 * TW)]).then_inc(pair_loaded[f % WB], 16)
                elif kind == "store_tile":
                    f = s[1]
                    sp.wait_ge(y_ready, f + 1)
                    sp.dma_start(sorted_y[f * P:(f + 1) * P, :], y_sb[:, f % 2, :]).then_inc(y_stored[f % 2], 16)
                elif kind == "finish":
                    b = s[1]
                    if b == 0:
                        sp.wait_ge(y_ready, FT)
                        for bb in range(2):
                            sp.dma_start(x_again[:, bb, :, :], x_v[bb]).then_inc(x_reloaded[bb], 16)
                    sp.wait_ge(out_ready, b + 1)
                    sp.dma_start(out_v[b], s_sb[:, C * b:C * b + C, :]).then_inc(out_stored, 16)
                    if b + 2 < B:
                        sp.dma_start(x_again[:, b % 2, :, :], x_v[b + 2]).then_inc(x_reloaded[b + 2], 16)
            sp.wait_ge(out_stored, 16 * B)

        @block.gpsimd
        def _(pool):
            chain = [0]

            def link(ins):
                chain[0] += 1
                ins.then_inc(pool_chain, 1)
                pool.wait_ge(pool_chain, chain[0])

            g = nc.gpsimd
            link(g.memset(ident[:, :], 0.0))
            link(g.affine_select(out=ident[:, :], in_=ident[:, :], compare_op=ALU.not_equal, fill=1.0,
                                 base=0, pattern=[[-1, P]], channel_multiplier=1))
            link(g.memset(ones[:, :], 1.0))
            link(g.affine_select(out=before[:, :], in_=ones[:, :], compare_op=ALU.is_gt, fill=0.0,
                                 base=0, pattern=[[1, P]], channel_multiplier=-1))
            g.memset(neg_half[:, :], -0.5).then_inc(consts_ready, 1)
            link(g.iota(iota_i[:, :], pattern=[[1, 40]], base=0, channel_multiplier=0))
            g.tensor_copy(iota[:, :], iota_i[:, :]).then_inc(iota_ready, 1)
            for s in steps:
                kind = s[0]
                if kind == "norm":
                    b = s[1]
                    if b == 0:
                        pool.wait_ge(consts_ready, 1)
                    pool.wait_ge(stats_ready, b + 1)
                    if b >= 2:
                        pool.wait_ge(xn_ready, b - 1)
                    link(g.tensor_scalar(var_eps[:, :], mv[:, b % 2, :, 1], EPS, None, ALU.add))
                    link(g.tensor_tensor(rstd[:, b % 2, :], var_eps[:, :], neg_half[:, :], ALU.pow))
                    link(g.tensor_scalar(shift[:, b % 2, :], mv[:, b % 2, :, 0], -1.0, None, ALU.mult))
                    g.tensor_tensor(shift[:, b % 2, :], shift[:, b % 2, :], rstd[:, b % 2, :],
                                    ALU.mult).then_inc(rstd_ready, 1)
                elif kind == "project" and s[1] >= 2:
                    b, i = s[1:]
                    n = 2 * b + i
                    pool.wait_ge(rest_ready, n + 1)
                    if b >= 1:
                        pool.wait_ge(stacked[(b - 1) % STK], 12 * 16 * ((b - 1) // STK + 1))
                    g.tensor_copy(parts[:, i, 1, :], rest[:, i, :]).then_inc(mid_ready, 1)
                    pool.wait_ge(mid_ready, n + 1)
                    g.tensor_tensor(parts[:, i, 2, :], rest[:, i, :], parts[:, i, 1, :],
                                    ALU.subtract).then_inc(low_ready, 1)
                elif kind == "norm_o":
                    b = s[1]
                    pool.wait_ge(stats_o_ready, b + 1)
                    if b >= 1:
                        pool.wait_ge(z_ready, b)
                    link(g.tensor_scalar(var_eps_o[:, :], mv_o[:, :, 1], EPS, None, ALU.add))
                    link(g.tensor_tensor(rstd_o[:, :], var_eps_o[:, :], neg_half[:, :], ALU.pow))
                    link(g.tensor_scalar(shift_o[:, :], mv_o[:, :, 0], -1.0, None, ALU.mult))
                    g.tensor_tensor(shift_o[:, :], shift_o[:, :], rstd_o[:, :], ALU.mult).then_inc(rstd_o_ready, 1)
                elif kind == "scatter":
                    pool.wait_ge(sorted_zeroed, 16)
                    pool.wait_ge(slots_ready, 1)
                    pool.wait_ge(xn_ready, B)
                    for t in range(NT):
                        pool.indirect_dma_start(
                            sorted_x, bass.IndirectOffsetOnAxis(ap=slot[:, t:t + 1], axis=0),
                            xn[:, t, :], None).then_inc(scattered, 16)
                elif kind == "gather":
                    if s[1] == 0:
                        for i in range(2):
                            pool.wait_ge(y_stored[i], 16 * len(range(i, FT, 2)))
                        pool.wait_ge(scattered, 16 * NT)
                    for t in range(C * s[1], C * s[1] + C):
                        pool.indirect_dma_start(
                            yg[:, t, :], None, sorted_y,
                            bass.IndirectOffsetOnAxis(ap=slot[:, t:t + 1], axis=0)).then_inc(gathered[t // C], 16)

        @block.scalar
        def _(act):
            a = nc.scalar
            act.dma_start(lams[:, 0, :], row(lq1).to_broadcast([P, HD])).then_inc(lam_dots, 16)
            act.dma_start(lams[:, 1, :], row(lq2).to_broadcast([P, HD])).then_inc(lam_dots, 16)
            act.dma_start(lams[:, 2, :], row(lk1).to_broadcast([P, HD])).then_inc(lam_dots, 16)
            act.dma_start(lams[:, 3, :], row(lk2).to_broadcast([P, HD])).then_inc(lam_dots, 16)
            def load_experts():
                tab = table[:, :].rearrange("p (e w) -> p e w", e=EXP + 1)
                act.dma_start(b1_rows[:, :], b1.rearrange("e (c p) -> (e c) p", p=P)).then_inc(b1_loaded, 16)
                for e0, n in ((0, EXP), (EXP, 1)):
                    act.dma_start(tab[:, e0:e0 + n, T_B2:T_B2 + D],
                                  b2[0:n].unsqueeze(0).to_broadcast([P, n, D])).then_inc(expert_loaded, 16)
                    act.dma_start(tab[:, e0:e0 + n, T_W1:T_W1 + FF],
                                  w1[0:n].rearrange("e p n -> p e n")).then_inc(expert_loaded, 16)
                    act.dma_start(w2_sb[:, e0 * FF:(e0 + n) * FF].rearrange("p (m n) -> p m n", n=D),
                                  w2[0:n].rearrange("e (c p) n -> p (e c) n", p=P)).then_inc(expert_loaded, 16)
            act.wait_ge(lam_dots, 65)
            a.activation(lam_exp[:, :], lam_dot[:, :], ACT.Exp).then_inc(lam_exps, 1)
            for s in steps:
                kind = s[0]
                shared = ring[uses[s] % RING] if s in uses else None
                if kind == "norm":
                    b = s[1]
                    act.wait_ge(rstd_ready, b + 1)
                    for c in range(C):
                        last = a.activation(xn[:, C * b + c, :], xin[:, C * b + c, :], ACT.Identity,
                                            bias=shift[:, b % 2, c:c + 1], scale=rstd[:, b % 2, c:c + 1])
                    last.then_inc(xn_ready, 1)
                    if b == B - 1:
                        load_experts()
                elif kind == "project":
                    b, i = s[1:]
                    act.wait_ge(shared_filled, uses[s] + 1)
                    if b >= 1:
                        act.wait_ge(stacked[(b - 1) % STK], 12 * 16 * ((b - 1) // STK + 1))
                    a.activation(parts[:, i, 0, :], shared[:, :], ACT.Identity,
                                 bias=qk_bias[:, i:i + 1]).then_inc(high_ready, 1)
                    if b < 2:
                        act.wait_ge(rest_ready, 2 * b + i + 1)
                        a.activation(parts[:, i, 1, :], rest[:, i, :], ACT.Copy).then_inc(mid_ready, 1)
                elif kind == "exp":
                    n = s[1]
                    act.wait_ge(exp_filled, n + 1)
                    if n >= PR:
                        act.wait_ge(pv_done, (n - PR) // 4 + 1)
                    a.activation(probs[:, n % PR, :], exp_bank[n % 2][:, :], ACT.Exp,
                                 scale=SCALE).then_inc(exp_done, 1)
                elif kind == "copy_o":
                    grp = s[1]
                    act.wait_ge(pv_done, 4 * grp + 4)
                    if grp >= 2:
                        act.wait_ge(shared_filled, uses[("turn_o", grp - 2)] + 1)
                    a.activation(oT[:, grp % 2, :], pv_bank[:, :], ACT.Copy).then_inc(o_copied, 1)
                elif kind == "turn_z":
                    act.wait_ge(shared_filled, uses[s] + 1)
                    if s[1] >= 1:
                        act.wait_ge(s_ready, s[1])
                    a.activation(zT[:, :], shared[:, :], ACT.Copy).then_inc(zT_ready, 1)
                elif kind == "hidden" and s[2] == 0:
                    f = s[1]
                    act.wait_ge(shared_filled, uses[s] + 1)
                    if f >= 2:
                        act.wait_ge(shared_filled, uses[("down", f - 2)] + 1)
                    for c in range(FC):
                        last = a.activation(hT[:, f % 2, c, :], shared[:, c * P:(c + 1) * P], ACT.Relu,
                                            bias=pair[:, f % WB, T_B1 + c:T_B1 + c + 1])
                    last.then_inc(hid_ready[0], 1)
                elif kind == "gate":
                    for half in range(2):
                        for b in range(B // 2 * half, B // 2 * (half + 1)):
                            act.wait_ge(gathered[b], 16 * C)
                        part = yg[:, NT // 2 * half:NT // 2 * (half + 1), :]
                        a.activation(part, part, ACT.Silu, scale=0.5).then_inc(gate_ready, 1)

        @block.vector
        def _(dve):
            v = nc.vector
            chain = [0]

            def link(ins):
                chain[0] += 1
                ins.then_inc(dve_chain, 1)
                dve.wait_ge(dve_chain, chain[0])

            v.memset(ones_bf[:, :], 1.0)
            v.memset(zeros, 0.0)
            link(v.memset(va[:, :, :, :, HD:VW], 0.0))
            v.memset(va[:, :, :, :, HD:HD + 1], 1.0).then_inc(dve_consts, 1)

            def fold():
                dve.wait_ge(lam_dots, 64)
                link(v.tensor_tensor(lam_prod[:, :, :], lams[:, 0:2, :], lams[:, 2:4, :], ALU.mult))
                v.tensor_reduce(lam_dot[:, :], lam_prod[:, :, :], AX.X, ALU.add).then_inc(lam_dots, 1)
                dve.wait_ge(lam_exps, 1)
                link(v.tensor_tensor(neg_lam[:, :], lam_exp[:, 1:2], lam_exp[:, 0:1], ALU.subtract))
                link(v.tensor_scalar(neg_lam[:, :], neg_lam[:, :], -LAM_INIT, None, ALU.add))
                dve.wait_ge(small_loaded, 16 * SMALL)
                for i, w in enumerate((wq_sb, wk_sb)):
                    v.tensor_copy(wqk[:, i, :].rearrange("p (d h) -> p h d", d=HD),
                                  w[:, :].rearrange("p (h d) -> p h d", d=HD))
                w = HALF * HD
                v.scalar_tensor_tensor(wv_eff[:, :], wv_sb[:, w:2 * w], neg_lam[:, 0:1], wv_sb[:, 0:w],
                                       ALU.mult, ALU.add)
                v.scalar_tensor_tensor(bv_eff[:, :], bv_sb[:, w:2 * w], neg_lam[:, 0:1], bv_sb[:, 0:w],
                                       ALU.mult, ALU.add)
                link(v.tensor_scalar(wo_eff[:, :], wo_sb[:, :], lnw_sb[:, 0:1], OUT_SCALE, ALU.mult, ALU.mult))
                dve.wait_ge(consts_ready, 1)
                v.tensor_copy(ident_bf[:, :], ident[:, :])
                v.tensor_scalar(lnb_wide[:, :], ones[:, :], lnb_sb[:, 0:1], OUT_SCALE,
                                ALU.mult, ALU.mult).then_inc(folded, 1)
                dve.wait_ge(shared_filled, 1)
                link(v.tensor_tensor(bo_eff[:, :], ring[0][:, 0:D], bo_sb[:, :], ALU.add))
                v.memset(v01[:, 0:1], 0.0).then_inc(shared_free, 1)

            def build_table():
                dve.wait_ge(expert_loaded, 16 * 6)
                tab = table[:, :].rearrange("p (e w) -> p e w", e=EXP + 1)
                v.tensor_tensor(tab[:, 0:EXP, T_B2:T_B2 + D], tab[:, 0:EXP, T_B2:T_B2 + D],
                                tab[:, 1:EXP + 1, T_B2:T_B2 + D], ALU.add).then_inc(table_ready, 1)

            def route(use, shared):
                dve.wait_ge(xn_ready, B)
                dve.wait_ge(iota_ready, 1)
                link(v.tensor_tensor(v01[:, :], xn[:, :, 0], xn[:, :, 1], ALU.add))
                link(v.scalar_tensor_tensor(v_abs[:, :], v01[:, :], -1.0, v01[:, :], ALU.mult, ALU.max))
                c3 = cmp[:, 0:NT * 15].rearrange("p (t k) -> p t k", k=15)
                link(v.tensor_tensor(c3, v_abs[:, :].unsqueeze(2).to_broadcast([P, NT, 15]),
                                     iota[:, 1:16].unsqueeze(1).to_broadcast([P, NT, 15]), ALU.is_ge))
                link(v.tensor_reduce(n_abs[:, :], c3, AX.X, ALU.add))
                link(v.tensor_scalar(sign[:, :], v01[:, :], 0.0, 2.0, ALU.is_ge, ALU.mult))
                link(v.scalar_tensor_tensor(h[:, :], sign[:, :], -1.0, n_abs[:, :], ALU.add, ALU.mult))
                v.tensor_scalar(wrap[:, 0, :], h[:, :], 0.0, 8.0, ALU.is_lt, ALU.mult)
                v.tensor_scalar(wrap[:, 1, :], h[:, :], -8.0, 8.0, ALU.is_lt, ALU.mult)
                link(v.tensor_scalar(wrap[:, 2, :], h[:, :], 8.0, -8.0, ALU.is_ge, ALU.mult))
                for i in range(3):
                    link(v.tensor_tensor(h[:, :], h[:, :], wrap[:, i, :], ALU.add))
                link(v.tensor_tensor(onehot[:, :, :], h[:, :].unsqueeze(1).to_broadcast([P, EXP, NT]),
                                     iota[:, 0:EXP].unsqueeze(2).to_broadcast([P, EXP, NT]), ALU.is_equal))
                v.tensor_reduce(count[:, :], onehot[:, :, :], AX.X, ALU.add).then_inc(count_ready, 1)
                flat = work[:, 768:1024]
                link(v.tensor_tensor_scan(flat, work[:, 512:768], zeros,
                                          0.0, ALU.add, ALU.add))
                link(v.tensor_tensor(seen[:, :, :], seen[:, :, :], onehot[:, :, :], ALU.subtract))
                dve.wait_ge(shared_filled, use + 1)
                c2 = cmp[:, 0:EXP * NT].rearrange("p (e k) -> p e k", k=NT)
                link(v.tensor_scalar(tile_base[:, :], shared[:, EXP:2 * EXP], 1.0 / P, None, ALU.mult))
                link(v.tensor_tensor(c2, tile_base[:, :].unsqueeze(2).to_broadcast([P, EXP, NT]),
                                     iota[:, 0:NT].unsqueeze(1).to_broadcast([P, EXP, NT]), ALU.is_gt))
                link(v.tensor_reduce(tiles_of[:, :], c2, AX.X, ALU.add))
                link(v.tensor_tensor_scan(tile_end[:, :], tiles_of[:, :], zeros[:, 0:EXP], 0.0, ALU.add, ALU.add))
                link(v.tensor_tensor(tile_base[:, :], tile_end[:, :], tiles_of[:, :], ALU.subtract))
                link(v.scalar_tensor_tensor(base[:, :], tile_base[:, :], float(P), shared[:, 0:EXP],
                                            ALU.mult, ALU.add))
                link(v.tensor_tensor(base[:, :], base[:, :], seen[:, :, 0], ALU.subtract))
                link(v.tensor_tensor(seen[:, :, :], seen[:, :, :],
                                     base[:, :].unsqueeze(2).to_broadcast([P, EXP, NT]), ALU.add))
                link(v.tensor_tensor(seen[:, :, :], seen[:, :, :], onehot[:, :, :], ALU.mult))
                link(v.tensor_reduce(slot_f[:, :], seen[:, :, :].rearrange("p e t -> p t e"), AX.X, ALU.add))
                v.tensor_copy(slot[:, :], slot_f[:, :]).then_inc(slots_ready, 1)
                c1 = cmp[:, 0:FT * (EXP - 1)].rearrange("p (f e) -> p f e", e=EXP - 1)
                link(v.tensor_tensor(c1, iota[:, 0:FT].unsqueeze(2).to_broadcast([P, FT, EXP - 1]),
                                     tile_base[:, 1:EXP].unsqueeze(1).to_broadcast([P, FT, EXP - 1]), ALU.is_ge))
                link(v.tensor_reduce(texp_f[:, :], c1, AX.X, ALU.add))
                v.tensor_copy(texp[:, :], texp_f[:, :]).then_inc(texp_ready, 1)
                v.memset(v01[:, 0:1], 0.0).then_inc(shared_free, 1)

            for s in steps:
                kind = s[0]
                shared = ring[uses[s] % RING] if s in uses else None
                if kind == "norm":
                    b = s[1]
                    dve.wait_ge(x_loaded[b], 16)
                    if b >= 1:
                        dve.wait_ge(stats_ready, b)
                    if b >= 2:
                        dve.wait_ge(rstd_ready, b - 1)
                    for c in range(C):
                        last = v.bn_stats(stats[:, c, :], xin[:, C * b + c, :])
                    link(last)
                    for c in range(C):
                        last = v.bn_aggr(mv[:, b % 2, c, :], stats[:, c, :])
                    last.then_inc(stats_ready, 1)
                elif kind == "transpose_x":
                    b = s[1]
                    dve.wait_ge(shared_filled, uses[s] + 1)
                    if b >= 2:
                        dve.wait_ge(shared_filled, uses[("values", b - 2)] + 1)
                    v.tensor_copy(xT[:, b % 2, :], shared[:, :]).then_inc(xT_ready, 1)
                elif kind == "project":
                    b, i = s[1:]
                    dve.wait_ge(high_ready, 2 * b + i + 1)
                    if b >= 1:
                        dve.wait_ge(low_ready, 2 * b + i - 1)
                    v.scalar_tensor_tensor(rest[:, i, :], shared[:, :], qk_bias[:, i:i + 1], parts[:, i, 0, :],
                                           ALU.add, ALU.subtract).then_inc(rest_ready, 1)
                    if b < 2:
                        dve.wait_ge(mid_ready, 2 * b + i + 1)
                        v.tensor_tensor(parts[:, i, 2, :], rest[:, i, :], parts[:, i, 1, :],
                                        ALU.subtract).then_inc(low_ready, 1)
                elif kind == "values":
                    b = s[1]
                    dve.wait_ge(shared_filled, uses[s] + 1)
                    if b >= 2:
                        dve.wait_ge(pv_done, 8 * (b - 1))
                    w = HALF * HD
                    v.tensor_tensor(va[:, b % 2, :, :, 0:HD],
                                    shared[:, 0:C * w].rearrange("p (c i d) -> p c i d", c=C, d=HD),
                                    bv_eff[:, :].rearrange("p (i d) -> p i d", d=HD).unsqueeze(1)
                                    .to_broadcast([P, C, HALF, HD]), ALU.add).then_inc(va_ready, 1)
                elif kind == "score":
                    n = s[1]
                    b, col = divmod(n, HEADS * C)
                    dve.wait_ge(score_filled, n + 1)
                    if col == 0 and b >= 2:
                        dve.wait_ge(max_split, 2 * (b - 1))
                    v.tensor_reduce(neg_max[:, b % 2, col:col + 1], score_bank[n % 2][:, :], AX.X, ALU.max,
                                    negate=True).then_inc(max_taken, 1)
                elif kind == "split_max":
                    grp = s[1]
                    b, g2 = divmod(grp, 2)
                    dve.wait_ge(max_taken, 16 * (grp + 1))
                    if grp >= 2:
                        dve.wait_ge(shared_filled, uses[("turn_max", grp - 2)] + 1)
                    part = [max_parts[:, g2, j, :] for j in range(PARTS)]
                    whole = neg_max[:, b % 2, 16 * g2:16 * g2 + 16]
                    link(v.tensor_copy(part[0], whole))
                    link(v.tensor_tensor(max_rest[:, g2, :], whole, part[0], ALU.subtract))
                    link(v.tensor_copy(part[1], max_rest[:, g2, :]))
                    v.tensor_tensor(part[2], max_rest[:, g2, :], part[1], ALU.subtract).then_inc(max_split, 1)
                elif kind == "turn_max":
                    grp = s[1]
                    dve.wait_ge(shared_filled, uses[s] + 1)
                    if grp >= 2:
                        dve.wait_ge(max_stacked, 16 * (grp - 1))
                    v.tensor_copy(max_rows[:, grp % 2, :], shared[0:PARTS * 16, 0:P // 2].bitcast(BF16)).then_inc(max_turned, 1)
                elif kind == "b1":
                    dve.wait_ge(shared_filled, uses[s] + 1)
                    tab = table[:, :].rearrange("p (e w) -> p e w", e=EXP + 1)
                    rows = shared[:, 0:EXP * FC].rearrange("p (e c) -> p e c", c=FC)
                    v.tensor_copy(tab[:, 0:EXP, T_B1:T_B1 + FC], rows)
                    v.tensor_copy(tab[:, EXP, T_B1:T_B1 + FC], rows[:, 0, :]).then_inc(b1_ready, 1)
                elif kind == "turn_o":
                    grp = s[1]
                    b, g2 = divmod(grp, 2)
                    dve.wait_ge(shared_filled, uses[s] + 1)
                    if grp >= 4:
                        dve.wait_ge(z_ready, b - 1)
                    o4 = shared[:, :].rearrange("p (c i w) -> p c i w", c=C, w=VW)
                    link(v.reciprocal(inv_sum[:, :], shared[:, :].rearrange("p (n w) -> p n w", w=VW)[:, :, HD]))
                    v.tensor_tensor(attn[:, b % 2, :, g2 * HALF * HD:(g2 + 1) * HALF * HD]
                                    .rearrange("p c (i d) -> p c i d", d=HD), o4[:, :, :, 0:HD],
                                    inv_sum[:, :].rearrange("p (c i) -> p c i", c=C).unsqueeze(3)
                                    .to_broadcast([P, C, HALF, HD]), ALU.mult).then_inc(attn_ready, 1)
                elif kind == "norm_o":
                    b = s[1]
                    dve.wait_ge(attn_ready, 2 * b + 2)
                    if b >= 1:
                        dve.wait_ge(z_ready, b)
                    for c in range(C):
                        last = v.bn_stats(stats_o[:, c, :], attn[:, b % 2, c, :])
                    link(last)
                    for c in range(C):
                        last = v.bn_aggr(mv_o[:, c, :], stats_o[:, c, :])
                    last.then_inc(stats_o_ready, 1)
                elif kind == "scale_o":
                    b = s[1]
                    dve.wait_ge(rstd_o_ready, b + 1)
                    if b >= 1:
                        dve.wait_ge(shared_filled, uses[("turn_z", b - 1)] + 1)
                    for c in range(C):
                        last = v.tensor_scalar(z[:, c, :], attn[:, b % 2, c, :], rstd_o[:, c:c + 1],
                                               shift_o[:, c:c + 1], ALU.mult, ALU.add)
                    last.then_inc(z_ready, 1)
                elif kind == "project_o":
                    b = s[1]
                    dve.wait_ge(shared_filled, uses[s] + 1)
                    dve.wait_ge(xn_ready, b + 1)
                    v.tensor_tensor(s_sb[:, C * b:C * b + C, :], shared[:, :].rearrange("p (c n) -> p c n", c=C),
                                    bo_eff[:, :].unsqueeze(1).to_broadcast([P, C, D]), ALU.add).then_inc(s_ready, 1)
                elif kind == "fold":
                    fold()
                elif kind == "table":
                    build_table()
                elif kind == "route":
                    route(uses[s], shared)
                elif kind == "turn_tile":
                    f = s[1]
                    dve.wait_ge(shared_filled, uses[s] + 1)
                    if f >= 2:
                        dve.wait_ge(shared_filled, uses[("hidden", f - 2, 1)] + 1)
                    v.tensor_copy(xsT[:, f % 2, :], shared[:, 0:P]).then_inc(xsT_ready, 1)
                elif kind == "hidden" and s[2] == 1:
                    f = s[1]
                    dve.wait_ge(shared_filled, uses[s] + 1)
                    if f >= 2:
                        dve.wait_ge(shared_filled, uses[("down", f - 2)] + 1)
                    for c in range(FC):
                        last = v.tensor_scalar(hT[:, f % 2, FC + c, :], shared[:, c * P:(c + 1) * P],
                                               pair[:, f % WB, TW + T_B1 + c:TW + T_B1 + c + 1], 0.0,
                                               ALU.add, ALU.max)
                    last.then_inc(hid_ready[1], 1)
                elif kind == "down":
                    f = s[1]
                    dve.wait_ge(shared_filled, uses[s] + 1)
                    if f >= 2:
                        dve.wait_ge(y_stored[f % 2], 16 * (f // 2))
                    v.tensor_tensor(y_sb[:, f % 2, :], shared[:, 0:D], pair[:, f % WB, T_B2:T_B2 + D],
                                    ALU.add).then_inc(y_ready, 1)
                elif kind == "finish":
                    b = s[1]
                    dve.wait_ge(gate_ready, 1 if b < B // 2 else 2)
                    dve.wait_ge(x_reloaded[b], 16)
                    dve.wait_ge(s_ready, b + 1)
                    tok = slice(C * b, C * b + C)
                    link(v.tensor_tensor(s_sb[:, tok, :], s_sb[:, tok, :], yg[:, tok, :], ALU.mult))
                    v.tensor_tensor(s_sb[:, tok, :], s_sb[:, tok, :], x_again[:, b % 2, :, :],
                                    ALU.add).then_inc(out_ready, 1)

        @block.tensor
        def _(pe):
            t = nc.tensor

            def free(use):
                if use >= RING:
                    pe.wait_ge(*reader[use - RING])

            reader = {0: (shared_free, 1)}
            for s, use in uses.items():
                kind = s[0]
                reader[use] = {
                    "transpose_x": lambda: (xT_ready, s[1] + 1),
                    "project": lambda: (rest_ready, 2 * s[1] + s[2] + 1),
                    "values": lambda: (va_ready, s[1] + 1),
                    "turn_max": lambda: (max_turned, s[1] + 1),
                    "b1": lambda: (b1_ready, 1),
                    "turn_o": lambda: (attn_ready, s[1] + 1),
                    "turn_z": lambda: (zT_ready, s[1] + 1),
                    "project_o": lambda: (s_ready, s[1] + 1),
                    "route": lambda: (shared_free, 2),
                    "turn_tile": lambda: (xsT_ready, s[1] + 1),
                    "down": lambda: (y_ready, s[1] + 1),
                    "hidden": lambda: (hid_ready[s[2]], s[1] + 1),
                }[kind]()

            pe.wait_ge(folded, 1)
            pe.wait_ge(consts_ready, 1)
            t.matmul(ring[0][:, 0:D], lnb_wide[:, :], wo_sb[:, :], start=True, stop=True).then_inc(shared_filled, 1)
            expert = [None] * FT
            for s in steps:
                kind = s[0]
                shared = ring[uses[s] % RING] if s in uses else None
                if kind == "transpose_x":
                    b = s[1]
                    pe.wait_ge(xn_ready, b + 1)
                    free(uses[s])
                    for c in range(C):
                        last = t.transpose(shared[:, c * P:(c + 1) * P], xn[:, C * b + c, :], ident[:, :])
                    last.then_inc(shared_filled, 1)
                elif kind == "project":
                    b, i = s[1:]
                    if i == 0:
                        pe.wait_ge(xT_ready, b + 1)
                    free(uses[s])
                    t.matmul(shared[:, :], wqk[:, i, :], xT[:, b % 2, :], start=True, stop=True).then_inc(shared_filled, 1)
                elif kind == "values":
                    b = s[1]
                    free(uses[s])
                    w = HALF * HD
                    for c in range(C):
                        last = t.matmul(shared[:, c * w:(c + 1) * w], xT[:, b % 2, c * P:(c + 1) * P], wv_eff[:, :],
                                        start=True, stop=True)
                    last.then_inc(shared_filled, 1)
                elif kind == "score":
                    n = s[1]
                    b, col = divmod(n, HEADS * C)
                    hh, c = divmod(col, C)
                    if col == 0:
                        pe.wait_ge(stacked[b % STK], 12 * 16 * (b // STK + 1))
                    if n >= 2:
                        pe.wait_ge(max_taken, n - 1)
                    t.matmul(score_bank[n % 2][:, :], qs[0:MAX_ROW, b % STK, hh, c * P:(c + 1) * P],
                             ks[0:MAX_ROW, b % STK, hh, :], start=True, stop=True).then_inc(score_filled, 1)
                elif kind == "turn_max":
                    grp = s[1]
                    pe.wait_ge(max_split, grp + 1)
                    free(uses[s])
                    t.transpose(shared[0:PARTS * 16, 0:P // 2].bitcast(BF16),
                                max_parts[:, grp % 2, :, :].rearrange("p j n -> p (j n)"),
                                ident_bf[:, :]).then_inc(shared_filled, 1)
                elif kind == "b1":
                    pe.wait_ge(b1_loaded, 16)
                    free(uses[s])
                    t.transpose(shared[:, 0:EXP * FC], b1_rows[:, :], ident[0:EXP * FC, 0:EXP * FC]).then_inc(shared_filled, 1)
                elif kind == "exp":
                    n = s[1]
                    b, r = divmod(n, HEADS * C)
                    g2, r = divmod(r, C * HALF)
                    kc, i = divmod(r, HALF)
                    hh = g2 * HALF + i
                    if n % 16 == 0:
                        pe.wait_ge(max_stacked, 16 * (n // 16 + 1))
                        if n == 0:
                            pe.wait_ge(ones_stacked, 16 * STK)
                    if n >= 2:
                        pe.wait_ge(exp_done, n - 1)
                    t.matmul(exp_bank[n % 2][:, :], ks[0:KROWS, b % STK, hh, kc * P:(kc + 1) * P],
                             qs[0:KROWS, b % STK, hh, :], start=True, stop=True).then_inc(exp_filled, 1)
                elif kind == "pv":
                    n4 = s[1]
                    grp, kc = divmod(n4, C)
                    b = grp // 2
                    pe.wait_ge(exp_done, 4 * n4 + 4)
                    if n4 % (2 * C) == 0:
                        pe.wait_ge(va_ready, b + 1)
                    if kc == 0 and grp >= 1:
                        pe.wait_ge(o_copied, grp)
                    for i in range(HALF):
                        last = t.matmul(pv_bank[VW * i:VW * (i + 1), :], va[:, b % 2, kc, i, :],
                                        probs[:, (4 * n4 + i) % PR, :], start=(kc == 0), stop=(kc == C - 1))
                    last.then_inc(pv_done, 1)
                elif kind == "turn_o":
                    grp = s[1]
                    pe.wait_ge(o_copied, grp + 1)
                    free(uses[s])
                    for c in range(C):
                        last = t.transpose(shared[:, c * P:(c + 1) * P], oT[:, grp % 2, c * P:(c + 1) * P], ident[:, :])
                    last.then_inc(shared_filled, 1)
                elif kind == "turn_z":
                    pe.wait_ge(z_ready, s[1] + 1)
                    free(uses[s])
                    for c in range(C):
                        last = t.transpose(shared[:, c * P:(c + 1) * P], z[:, c, :], ident[:, :])
                    last.then_inc(shared_filled, 1)
                elif kind == "project_o":
                    pe.wait_ge(zT_ready, s[1] + 1)
                    free(uses[s])
                    for c in range(C):
                        last = t.matmul(shared[:, c * D:(c + 1) * D], zT[:, c * P:(c + 1) * P], wo_eff[:, :],
                                        start=True, stop=True)
                    last.then_inc(shared_filled, 1)
                elif kind == "route":
                    pe.wait_ge(count_ready, 1)
                    free(uses[s])
                    t.matmul(shared[:, 0:EXP], before[:, :], count[:, :], start=True, stop=True)
                    t.matmul(shared[:, EXP:2 * EXP], ones[:, :], count[:, :], start=True, stop=True).then_inc(shared_filled, 1)
                elif kind == "turn_tile":
                    f = s[1]
                    pe.wait_ge(tile_loaded[f % 2], 16 * (f // 2 + 1))
                    free(uses[s])
                    t.transpose(shared[:, 0:P], xs[:, f % 2, :], ident[:, :]).then_inc(shared_filled, 1)
                elif kind == "hidden":
                    f, j = s[1:]
                    if j == 0:
                        pe.wait_ge(pair_loaded[f % WB], 16 * (f // WB + 1))
                        pe.wait_ge(xsT_ready, f + 1)
                    free(uses[s])
                    for c in range(FC):
                        o = j * TW + T_W1 + c * P
                        last = t.matmul(shared[:, c * P:(c + 1) * P], pair[:, f % WB, o:o + P], xsT[:, f % 2, :],
                                        start=True, stop=True)
                    last.then_inc(shared_filled, 1)
                elif kind == "down":
                    f = s[1]
                    e = pe.value_load(texp[0:1, f:f + 1], min_val=0, max_val=EXP - 1)
                    w2_at = [pe.snap(e * FF + k * D) for k in range(2 * FC)]
                    pe.wait_ge(hid_ready[0], f + 1)
                    pe.wait_ge(hid_ready[1], f + 1)
                    free(uses[s])
                    for k in range(2 * FC):
                        last = t.matmul(shared[:, 0:D], hT[:, f % 2, k, :], w2_sb[:, bass.ds(w2_at[k], D)],
                                        start=(k == 0), stop=(k == 2 * FC - 1))
                    last.then_inc(shared_filled, 1)


_INS = ["L0_attn_hidden_states", "L0_attn_Wq", "L0_attn_bq", "L0_attn_Wk", "L0_attn_bk", "L0_attn_Wv", "L0_attn_bv",
        "L0_attn_Wo", "L0_attn_bo", "L0_attn_lambda_q1", "L0_attn_lambda_k1", "L0_attn_lambda_q2",
        "L0_attn_lambda_k2", "L0_attn_ln_w", "L0_attn_ln_b", "L0_ffn_W1", "L0_ffn_b1", "L0_ffn_W2", "L0_ffn_b2"]
_OUTS = [((8, 512, 128), "float32")]


def kernel(**inputs):
    import numpy as _np
    import concourse.bacc as _bacc
    from concourse import mybir as _mybir
    from concourse.bass_utils import run_bass_kernel_spmd as _run

    nc = _bacc.Bacc("TRN2", target_bir_lowering=False, num_devices=1)
    arrays, args = {}, []
    for name in _INS:
        a = _np.ascontiguousarray(inputs[name])
        arrays[f"in_{name}_dram"] = a
        args.append(nc.dram_tensor(f"in_{name}_dram", a.shape, _mybir.dt.from_np(a.dtype), kind="ExternalInput").ap())
    for i, (shape, dtype) in enumerate(_OUTS):
        dt = _mybir.dt.from_np(_np.dtype(dtype))
        args.append(nc.dram_tensor(f"out_{i}_dram", shape, dt, kind="ExternalOutput").ap())
    gated_attention_moe(nc, *args)
    r = _run(nc, [arrays], core_ids=[0])
    return r.results[0]["out_0_dram"]
```

```python
import concourse.bass as bass
from concourse import mybir
from contextlib import ExitStack

F32 = mybir.dt.float32
BF16 = mybir.dt.bfloat16
I32 = mybir.dt.int32
ALU = mybir.AluOpType
ACT = mybir.ActivationFunctionType
AX = mybir.AxisListType

P = 128
B, S, D = 8, 512, 128
HEADS, HD = 8, 16
HALF = HEADS // 2
C = S // P
NT = B * C
EXP = 8
FF = 4 * D
FC = FF // P
FT = NT + (EXP * (P - 1)) // P
LAM_INIT = 0.8
OUT_SCALE = 1.0 - LAM_INIT
EPS = 1e-5
SCALE = 1.0 / HD ** 0.5
PARTS = 3
Q_PART = [0, 1, 2, 0, 1, 0]
K_PART = [0, 0, 0, 1, 1, 2]
MAX_ROW = len(Q_PART) * HD
KROWS = MAX_ROW + PARTS
VW = 32
STK = 3
PR = 8
T_B2, T_W1, T_B1 = 0, D, D + FF
TW = D + FF + FC
LAG = 24
FFN_FIRST = 48.6
FFN_PACE = 4.0
H1, D0, D1 = 1.01, 3.0, 4.0
TT = 1.3
STATS_AT = (-31, -30.9, -27.5, -26.5, -26.4, -26.3, -25.4, -25.3)
NORM_AT = (-30, -29.8, -25.2, -25.19, -25.18, -25.17, -25.16, -25.15)
QKV_AT = (-27, 4, 40, 72, 104, 136, 168, 200)
GATHER_PACE = 3.9
EXP_OFF, PV_OFF = 0.2, 3.5
Z_SLACK = 4
FOLD_AT = 12
GATE_STEPS = 4
POOL_FINISH = (5, 6)
DVE_FINISH = tuple(b for b in range(B) if b not in POOL_FINISH)
FINISH_AT = (8.1, 8.2, 12.1, 12.2, 14.5, 8.1, 8.2, 18)
ROUTE_AT = (5.5, 10.5, 16.5)
RING = 3
WB = 3


def schedule():
    steps = []

    def at(time, *step):
        steps.append((time, len(steps), step))

    for b in range(B):
        at(STATS_AT[b], "stats", b)
        at(NORM_AT[b], "norm", b)
        qkv = QKV_AT[b]
        at(qkv, "transpose_x", b)
        at(qkv + 3 if b else -26, "project", b, 0)
        at(qkv + 7 if b else -25.9, "project", b, 1)
        at(qkv + 5 if b else -25.6, "split", b, 0)
        at(qkv + 9 if b else -25.5, "split", b, 1)
        at(32 * b + LAG - 27.8 if b else FOLD_AT + 0.2, "values", b)
        for j in range(4):
            at(qkv + (9.5, 11, 14, 15.5)[j] if b else -23 + 0.1 * j, "stack", b, j)
        for n in range(32 * b, 32 * b + 32):
            at(n, "score", n)
            at(n + LAG + EXP_OFF, "exp", n)
            if n % 4 == 3:
                at(n + LAG + PV_OFF, "pv", n // 4)
        for grp in (2 * b, 2 * b + 1):
            at(16 * grp + 15.5, "split_max", grp)
            at(16 * grp + 18.5, "turn_max", grp)
            at(16 * grp + LAG + 20, "copy_o", grp)
            at(16 * grp + LAG + 22.2, "turn_o", grp)
        at(32 * b + LAG + 39.5, "norm_o", b)
        slack = Z_SLACK if b < B - 1 else 0
        at(32 * b + LAG + 43.8 + slack, "scale_o", b)
        at(32 * b + LAG + 46.3 + slack, "turn_z", b)
        at(32 * b + LAG + 49.3 + slack, "project_o", b)
    at(-29.7, "fold_qk")
    at(0.5, "load_experts")
    at(FOLD_AT, "fold")
    at(FOLD_AT + 0.1, "bias_o")
    at(30.3, "b1")
    at(31.3, "table")
    for i in range(3):
        at(ROUTE_AT[i], "route", i)
    at(ROUTE_AT[1], "scatter")
    t = FFN_FIRST
    for f in range(FT):
        at(t - 6, "load_tile", f)
        at(t - TT, "turn_tile", f)
        at(t, "hidden", f, 0)
        at(t + H1, "hidden", f, 1)
        at(t + D0, "down_first", f)
        at(t + D1, "down", f)
        at(t + D1 + 0.5, "store_tile", f)
        t += FFN_PACE
    at(t + 1, "reload_x")
    for b in range(B):
        at(t + 2 + GATHER_PACE * b, "gather", b)
    last = 32 * B + LAG
    at(last + 4.5, "gate")
    for b in range(B):
        at(last + FINISH_AT[b], "finish", b)
    return [s for _, _, s in sorted(steps)]


def gated_attention_moe(nc, x, wq, bq, wk, bk, wv, bv, wo, bo, lq1, lk1, lq2, lk2,
                        ln_w, ln_b, w1, b1, w2, b2, out):
    steps = schedule()
    uses, fills = {}, {}
    for s in steps:
        if s == ("route", 1) or s[0] in ("transpose_x", "project", "values", "turn_max", "turn_o", "turn_z",
                                         "project_o", "bias_o", "b1", "turn_tile", "down_first", "hidden"):
            uses[s] = len(set(uses.values()))
        elif s[0] == "down":
            uses[s] = uses[("down_first", s[1])]
        if s in uses and s[0] != "down_first":
            fills[s] = len(fills) + 1

    x_v = x.rearrange("b (c p) d -> b p c d", p=P)
    out_v = out.rearrange("b (c p) d -> b p c d", p=P)
    sorted_x = nc.dram_tensor("sorted_x", (FT * P, D), F32, kind="Internal").ap()
    sorted_y = nc.dram_tensor("sorted_y", (FT * P, D), F32, kind="Internal").ap()

    ctx = ExitStack()
    with ctx:
        def sb(name, shape, dt=F32):
            return ctx.enter_context(nc.sbuf_tensor(name, shape, dt))

        def bank(name):
            return ctx.enter_context(nc.psum_tensor(name, [P, 512], F32))

        def sem(name):
            return ctx.enter_context(nc.semaphore(name))

        ident = sb("ident", [P, P])
        before = sb("before", [P, P])
        ones = sb("ones", [P, P])
        iota_i = sb("iota_i", [P, 40], I32)
        iota = sb("iota", [P, 40])
        neg_half = sb("neg_half", [P, C])
        wq_sb = sb("wq_sb", [P, D])
        wk_sb = sb("wk_sb", [P, D])
        wv_sb = sb("wv_sb", [P, D])
        wo_sb = sb("wo_sb", [P, D])
        wqk = sb("wqk", [P, 2, D])
        qk_bias = sb("qk_bias", [P, 2])
        bv_sb = sb("bv_sb", [P, D])
        bo_sb = sb("bo_sb", [P, D])
        lams = sb("lams", [P, 4, HD])
        lam_prod = sb("lam_prod", [P, 2, HD])
        lam_dot = sb("lam_dot", [P, 2])
        lam_exp = sb("lam_exp", [P, 2])
        neg_lam = sb("neg_lam", [P, 1])
        lnw_sb = sb("lnw_sb", [P, 1])
        lnb_sb = sb("lnb_sb", [P, 1])
        lnb_wide = sb("lnb_wide", [P, P])
        wv_eff = sb("wv_eff", [P, HALF * HD])
        bv_eff = sb("bv_eff", [P, HALF * HD])
        wo_eff = sb("wo_eff", [P, D])
        bo_eff = sb("bo_eff", [P, D])
        table = sb("table", [P, (EXP + 1) * TW])
        w2_sb = sb("w2_sb", [P, (EXP + 1) * FF])
        xn = sb("xn", [P, NT, D])
        yg = xn
        stats = sb("stats", [P, C, 6])
        mv = sb("mv", [P, 2, C, 2])
        var_eps = sb("var_eps", [P, C])
        rstd = sb("rstd", [P, 2, C])
        shift = sb("shift", [P, 2, C])
        xT = sb("xT", [P, 2, S])
        parts = sb("parts", [P, 2, PARTS, S], BF16)
        rest = sb("rest", [P, 2, S])
        qs = sb("qs", [P, STK, HEADS, S], BF16)
        ks = sb("ks", [P, STK, HEADS, S], BF16)
        va = sb("va", [P, 2, C, HALF, VW])
        neg_max = sb("neg_max", [P, 2, HEADS * C])
        max_parts = sb("max_parts", [P, 2, PARTS, 16], BF16)
        max_rest = sb("max_rest", [P, 2, 16])
        max_rows = sb("max_rows", [PARTS * 16, 2, P], BF16)
        ident_bf = sb("ident_bf", [P, P], BF16)
        ones_bf = sb("ones_bf", [PARTS, S], BF16)
        b1_rows = sb("b1_rows", [EXP * FC, P])
        probs = sb("probs", [P, PR, S])
        oT = sb("oT", [P, 2, S])
        inv_sum = sb("inv_sum", [P, C * HALF])
        attn = sb("attn", [P, 2, C, D])
        stats_o = sb("stats_o", [P, C, 6])
        mv_o = sb("mv_o", [P, C, 2])
        var_eps_o = sb("var_eps_o", [P, C])
        rstd_o = sb("rstd_o", [P, C])
        shift_o = sb("shift_o", [P, C])
        z = sb("z", [P, C, D])
        zT = sb("zT", [P, S])
        s_sb = sb("s_sb", [P, NT, D])
        xin = s_sb
        v01 = sb("v01", [P, NT])
        v_abs = sb("v_abs", [P, NT])
        n_abs = sb("n_abs", [P, NT])
        sign = sb("sign", [P, NT])
        h = sb("h", [P, NT])
        wrap = sb("wrap", [P, 3, NT])
        count = sb("count", [P, EXP])
        tiles_of = sb("tiles_of", [P, EXP])
        tile_end = sb("tile_end", [P, EXP])
        tile_base = sb("tile_base", [P, EXP])
        base = sb("base", [P, EXP])
        slot_f = sb("slot_f", [P, NT])
        slot = sb("slot", [P, NT], I32)
        texp_f = sb("texp_f", [P, FT])
        texp = sb("texp", [P, FT], I32)
        xs = sb("xs", [P, 2, D])
        xsT = sb("xsT", [P, 2, P])
        pair = sb("pair", [P, WB, 2 * TW])
        x_again = table[:, 0:NT * D].rearrange("p (t d) -> p t d", d=D)
        hT = sb("hT", [P, 2, 2 * FC, P])
        work = hT[:, :, :, :].rearrange("p a k n -> p (a k n)")
        cmp = work[:, 0:512]
        onehot = work[:, 512:768].rearrange("p (e t) -> p e t", e=EXP)
        seen = work[:, 768:1024].rearrange("p (e t) -> p e t", e=EXP)
        zeros = work[:, 1024:1024 + EXP * NT]
        y_sb = sb("y_sb", [P, 2, D])

        score_bank = [bank("score0"), bank("score1")]
        exp_bank = [bank("exp0"), bank("exp1")]
        pv_bank = bank("pv_bank")
        ring = [bank(f"ring{i}") for i in range(RING)]

        consts_ready = sem("consts_ready")
        iota_ready = sem("iota_ready")
        dve_consts = sem("dve_consts")
        small_loaded = sem("small_loaded")
        expert_loaded = sem("expert_loaded")
        b1_loaded = sem("b1_loaded")
        lam_dots = sem("lam_dots")
        lam_exps = sem("lam_exps")
        folded = sem("folded")
        lnb_ready = sem("lnb_ready")
        qk_loaded = sem("qk_loaded")
        qk_folded = sem("qk_folded")
        bias_ready = sem("bias_ready")
        table_ready = sem("table_ready")
        x_loaded = [sem(f"x_loaded{b}") for b in range(B)]
        x_reloaded = [sem(f"x_reloaded{b}") for b in range(B)]
        stats_ready = sem("stats_ready")
        rstd_ready = sem("rstd_ready")
        xn_ready = sem("xn_ready")
        shared_filled = sem("shared_filled")
        counts_read = sem("counts_read")
        xT_ready = sem("xT_ready")
        high_ready = sem("high_ready")
        rest_ready = sem("rest_ready")
        mid_ready = sem("mid_ready")
        low_ready = sem("low_ready")
        stacked = [sem(f"stacked{i}") for i in range(STK)]
        parts_sent = sem("parts_sent")
        va_ready = sem("va_ready")
        score_filled = sem("score_filled")
        max_taken = sem("max_taken")
        max_split = sem("max_split")
        max_turned = sem("max_turned")
        max_stacked = sem("max_stacked")
        b1_ready = sem("b1_ready")
        ones_stacked = sem("ones_stacked")
        exp_filled = sem("exp_filled")
        exp_done = sem("exp_done")
        pv_done = sem("pv_done")
        o_copied = sem("o_copied")
        attn_ready = sem("attn_ready")
        stats_o_ready = sem("stats_o_ready")
        rstd_o_ready = sem("rstd_o_ready")
        z_ready = sem("z_ready")
        zT_ready = sem("zT_ready")
        s_ready = sem("s_ready")
        sorted_zeroed = sem("sorted_zeroed")
        slots_ready = sem("slots_ready")
        count_ready = sem("count_ready")
        seen_ready = sem("seen_ready")
        texp_ready = sem("texp_ready")
        scattered = sem("scattered")
        tile_loaded = [sem(f"tile_loaded{i}") for i in range(2)]
        pair_loaded = [sem(f"pair_loaded{i}") for i in range(WB)]
        xsT_ready = sem("xsT_ready")
        hid_ready = [sem(f"hid_ready{j}") for j in range(2)]
        y_ready = sem("y_ready")
        y_stored = [sem(f"y_stored{i}") for i in range(2)]
        gathered = [sem(f"gathered{b}") for b in range(B)]
        gate_ready = sem("gate_ready")
        out_ready = sem("out_ready")
        pool_out_ready = sem("pool_out_ready")
        out_stored = sem("out_stored")
        dve_chain = sem("dve_chain")
        pool_chain = sem("pool_chain")
        act_chain = sem("act_chain")

        block = ctx.enter_context(nc.Block())

        def row(ap):
            return ap.rearrange("(a n) -> a n", a=1)

        SMALL = 6

        def finish(eng, ops, b, link):
            eng.wait_ge(gate_ready, b * GATE_STEPS // B + 1)
            eng.wait_ge(x_reloaded[b], 16)
            eng.wait_ge(s_ready, b + 1)
            tok = slice(C * b, C * b + C)
            link(ops.tensor_tensor(s_sb[:, tok, :], s_sb[:, tok, :], yg[:, tok, :], ALU.mult))
            return ops.tensor_tensor(s_sb[:, tok, :], s_sb[:, tok, :], x_again[:, tok, :], ALU.add)

        @block.sync
        def _(sp):
            def load_x(b):
                sp.dma_start(xin[:, C * b:C * b + C, :], x_v[b]).then_inc(x_loaded[b], 16)

            load_x(0)
            sp.dma_start(wq_sb[:, :], wq).then_inc(qk_loaded, 16)
            sp.dma_start(wk_sb[:, :], wk).then_inc(qk_loaded, 16)
            load_x(1)
            for i, v in enumerate((bq, bk)):
                sp.dma_start(qk_bias[:, i:i + 1], v.rearrange("(h d) -> d h", d=HD),
                             allow_slow_non_contiguous=True).then_inc(qk_loaded, 16)
            for b in range(2, 5):
                load_x(b)
            sp.dma_start(wv_sb[:, :], wv).then_inc(small_loaded, 16)
            sp.dma_start(bv_sb[:, :], row(bv).to_broadcast([P, D])).then_inc(small_loaded, 16)
            for b in range(5, B):
                load_x(b)
            sp.dma_start(wo_sb[:, :], wo).then_inc(small_loaded, 16)
            sp.dma_start(bo_sb[:, :], row(bo).to_broadcast([P, D])).then_inc(small_loaded, 16)
            sp.dma_start(lnw_sb[:, :], ln_w.rearrange("(p a) -> p a", a=1)).then_inc(small_loaded, 16)
            sp.dma_start(lnb_sb[:, :], ln_b.rearrange("(p a) -> p a", a=1)).then_inc(small_loaded, 16)
            sp.wait_ge(dve_consts, 1)
            sp.dma_start(sorted_x.rearrange("(f p) d -> p f d", p=P),
                         zeros[:, 0:D].unsqueeze(1).to_broadcast([P, FT, D])).then_inc(sorted_zeroed, 16)
            for i in range(STK):
                sp.dma_start(ks[MAX_ROW:KROWS, i, :, :],
                             ones_bf[:, :].unsqueeze(1).to_broadcast([PARTS, HEADS, S])).then_inc(ones_stacked, 16)

            for s in steps:
                kind = s[0]
                if kind == "stack":
                    b, j = s[1:]
                    i, half = divmod(j, 2)
                    sp.wait_ge(low_ready, 2 * b + i + 1)
                    if b >= STK:
                        sp.wait_ge(exp_done, 32 * (b - STK + 1))
                    dst, order = ((qs, Q_PART), (ks, K_PART))[i]
                    for blk in range(3 * half, 3 * half + 3):
                        sp.dma_start(dst[blk * HD:(blk + 1) * HD, b % STK, :, :],
                                     parts[:, i, order[blk], :]).then_inc(stacked[b % STK], 16)
                elif kind == "turn_max":
                    grp = s[1]
                    b, g2 = divmod(grp, 2)
                    sp.wait_ge(max_turned, grp + 1)
                    sp.dma_start(qs[MAX_ROW:KROWS, b % STK, g2 * HALF:(g2 + 1) * HALF, :],
                                 max_rows[:, g2, :]).then_inc(max_stacked, 16)
                elif kind == "load_tile":
                    f = s[1]
                    if f == 0:
                        sp.wait_ge(scattered, 16 * NT)
                        sp.wait_ge(texp_ready, 1)
                        sp.wait_ge(table_ready, 1)
                        sp.wait_ge(b1_ready, 1)
                    if f >= 2:
                        sp.wait_ge(xsT_ready, f - 1)
                    sp.dma_start(xs[:, f % 2, :], sorted_x[f * P:(f + 1) * P, :]).then_inc(tile_loaded[f % 2], 16)
                    if f >= WB:
                        sp.wait_ge(y_ready, f - WB + 1)
                    e = sp.value_load(texp[0:1, f:f + 1], min_val=0, max_val=EXP - 1)
                    sp.dma_start(pair[:, f % WB, :], table[:, bass.ds(e * TW, 2 * TW)]).then_inc(pair_loaded[f % WB], 16)
                elif kind == "store_tile":
                    f = s[1]
                    sp.wait_ge(y_ready, f + 1)
                    sp.dma_start(sorted_y[f * P:(f + 1) * P, :], y_sb[:, f % 2, :]).then_inc(y_stored[f % 2], 16)
                elif kind == "reload_x":
                    for i in range(WB):
                        sp.wait_ge(pair_loaded[i], 16 * len(range(i, FT, WB)))
                    for b in range(B):
                        sp.dma_start(x_again[:, C * b:C * b + C, :], x_v[b]).then_inc(x_reloaded[b], 16)
                elif kind == "finish":
                    b = s[1]
                    if b in POOL_FINISH:
                        sp.wait_ge(pool_out_ready, POOL_FINISH.index(b) + 1)
                    else:
                        sp.wait_ge(out_ready, DVE_FINISH.index(b) + 1)
                    sp.dma_start(out_v[b], s_sb[:, C * b:C * b + C, :]).then_inc(out_stored, 16)
            sp.wait_ge(out_stored, 16 * B)

        @block.gpsimd
        def _(pool):
            chain = [0]

            def link(ins):
                chain[0] += 1
                ins.then_inc(pool_chain, 1)
                pool.wait_ge(pool_chain, chain[0])

            g = nc.gpsimd
            link(g.memset(ident[:, :], 0.0))
            link(g.affine_select(out=ident[:, :], in_=ident[:, :], compare_op=ALU.not_equal, fill=1.0,
                                 base=0, pattern=[[-1, P]], channel_multiplier=1))
            link(g.memset(ones[:, :], 1.0))
            link(g.affine_select(out=before[:, :], in_=ones[:, :], compare_op=ALU.is_gt, fill=0.0,
                                 base=0, pattern=[[1, P]], channel_multiplier=-1))
            g.memset(neg_half[:, :], -0.5).then_inc(consts_ready, 1)
            link(g.iota(iota_i[:, :], pattern=[[1, 40]], base=0, channel_multiplier=0))
            g.tensor_copy(iota[:, :], iota_i[:, :]).then_inc(iota_ready, 1)
            for s in steps:
                kind = s[0]
                if kind == "norm":
                    b = s[1]
                    if b == 0:
                        pool.wait_ge(consts_ready, 1)
                    pool.wait_ge(stats_ready, b + 1)
                    if b >= 2:
                        pool.wait_ge(xn_ready, b - 1)
                    link(g.tensor_scalar(var_eps[:, :], mv[:, b % 2, :, 1], EPS, None, ALU.add))
                    link(g.tensor_tensor(rstd[:, b % 2, :], var_eps[:, :], neg_half[:, :], ALU.pow))
                    link(g.tensor_scalar(shift[:, b % 2, :], mv[:, b % 2, :, 0], -1.0, None, ALU.mult))
                    g.tensor_tensor(shift[:, b % 2, :], shift[:, b % 2, :], rstd[:, b % 2, :],
                                    ALU.mult).then_inc(rstd_ready, 1)
                elif kind == "split" and s[1] >= 2:
                    b, i = s[1:]
                    n = 2 * b + i
                    pool.wait_ge(rest_ready, n + 1)
                    if b >= 1:
                        pool.wait_ge(stacked[(b - 1) % STK], 12 * 16 * ((b - 1) // STK + 1))
                    g.tensor_copy(parts[:, i, 1, :], rest[:, i, :]).then_inc(mid_ready, 1)
                    pool.wait_ge(mid_ready, n + 1)
                    g.tensor_tensor(parts[:, i, 2, :], rest[:, i, :], parts[:, i, 1, :],
                                    ALU.subtract).then_inc(low_ready, 1)
                elif kind == "norm_o":
                    b = s[1]
                    pool.wait_ge(stats_o_ready, b + 1)
                    if b >= 1:
                        pool.wait_ge(z_ready, b)
                    link(g.tensor_scalar(var_eps_o[:, :], mv_o[:, :, 1], EPS, None, ALU.add))
                    link(g.tensor_tensor(rstd_o[:, :], var_eps_o[:, :], neg_half[:, :], ALU.pow))
                    link(g.tensor_scalar(shift_o[:, :], mv_o[:, :, 0], -1.0, None, ALU.mult))
                    g.tensor_tensor(shift_o[:, :], shift_o[:, :], rstd_o[:, :], ALU.mult).then_inc(rstd_o_ready, 1)
                elif kind == "scatter":
                    pool.wait_ge(sorted_zeroed, 16)
                    pool.wait_ge(slots_ready, 1)
                    pool.wait_ge(xn_ready, B)
                    for t in range(NT):
                        pool.indirect_dma_start(
                            sorted_x, bass.IndirectOffsetOnAxis(ap=slot[:, t:t + 1], axis=0),
                            xn[:, t, :], None).then_inc(scattered, 16)
                elif kind == "finish" and s[1] in POOL_FINISH:
                    finish(pool, g, s[1], link).then_inc(pool_out_ready, 1)
                elif kind == "gather":
                    if s[1] == 0:
                        for i in range(2):
                            pool.wait_ge(y_stored[i], 16 * len(range(i, FT, 2)))
                        pool.wait_ge(scattered, 16 * NT)
                    for t in range(C * s[1], C * s[1] + C):
                        pool.indirect_dma_start(
                            yg[:, t, :], None, sorted_y,
                            bass.IndirectOffsetOnAxis(ap=slot[:, t:t + 1], axis=0)).then_inc(gathered[t // C], 16)

        @block.scalar
        def _(act):
            a = nc.scalar
            act.dma_start(lams[:, 0, :], row(lq1).to_broadcast([P, HD])).then_inc(lam_dots, 16)
            act.dma_start(lams[:, 1, :], row(lq2).to_broadcast([P, HD])).then_inc(lam_dots, 16)
            act.dma_start(lams[:, 2, :], row(lk1).to_broadcast([P, HD])).then_inc(lam_dots, 16)
            act.dma_start(lams[:, 3, :], row(lk2).to_broadcast([P, HD])).then_inc(lam_dots, 16)
            def load_experts():
                tab = table[:, :].rearrange("p (e w) -> p e w", e=EXP + 1)
                act.dma_start(b1_rows[:, :], b1.rearrange("e (c p) -> (e c) p", p=P)).then_inc(b1_loaded, 16)
                for e0, n in ((0, EXP), (EXP, 1)):
                    act.dma_start(tab[:, e0:e0 + n, T_B2:T_B2 + D],
                                  b2[0:n].unsqueeze(0).to_broadcast([P, n, D])).then_inc(expert_loaded, 16)
                    act.dma_start(tab[:, e0:e0 + n, T_W1:T_W1 + FF],
                                  w1[0:n].rearrange("e p n -> p e n")).then_inc(expert_loaded, 16)
                    act.dma_start(w2_sb[:, e0 * FF:(e0 + n) * FF].rearrange("p (m n) -> p m n", n=D),
                                  w2[0:n].rearrange("e (c p) n -> p (e c) n", p=P)).then_inc(expert_loaded, 16)
            for s in steps:
                kind = s[0]
                shared = ring[uses[s] % RING] if s in uses else None
                if kind == "norm":
                    b = s[1]
                    act.wait_ge(rstd_ready, b + 1)
                    for c in range(C):
                        last = a.activation(xn[:, C * b + c, :], xin[:, C * b + c, :], ACT.Identity,
                                            bias=shift[:, b % 2, c:c + 1], scale=rstd[:, b % 2, c:c + 1])
                    last.then_inc(xn_ready, 1)
                elif kind == "load_experts":
                    act.wait_ge(stacked[0], 12 * 16)
                    load_experts()
                elif kind == "fold":
                    act.wait_ge(lam_dots, 65)
                    a.activation(lam_exp[:, :], lam_dot[:, :], ACT.Exp).then_inc(lam_exps, 1)
                elif kind == "project":
                    b, i = s[1:]
                    act.wait_ge(shared_filled, fills[s])
                    if b == 0:
                        act.wait_ge(qk_loaded, 16 * 4)
                    if b >= 1:
                        act.wait_ge(stacked[(b - 1) % STK], 12 * 16 * ((b - 1) // STK + 1))
                    a.activation(parts[:, i, 0, :], shared[:, :], ACT.Identity,
                                 bias=qk_bias[:, i:i + 1]).then_inc(high_ready, 1)
                elif kind == "split" and s[1] < 2:
                    b, i = s[1:]
                    act.wait_ge(rest_ready, 2 * b + i + 1)
                    a.activation(parts[:, i, 1, :], rest[:, i, :], ACT.Copy).then_inc(mid_ready, 1)
                elif kind == "exp":
                    n = s[1]
                    act.wait_ge(exp_filled, n + 1)
                    if n >= PR:
                        act.wait_ge(pv_done, (n - PR) // 4 + 1)
                    a.activation(probs[:, n % PR, :], exp_bank[n % 2][:, :], ACT.Exp,
                                 scale=SCALE).then_inc(exp_done, 1)
                elif kind == "copy_o":
                    grp = s[1]
                    act.wait_ge(pv_done, 4 * grp + 4)
                    if grp >= 2:
                        act.wait_ge(shared_filled, fills[("turn_o", grp - 2)])
                    a.activation(oT[:, grp % 2, :], pv_bank[:, :], ACT.Copy).then_inc(o_copied, 1)
                elif kind == "turn_z":
                    act.wait_ge(shared_filled, fills[s])
                    if s[1] >= 1:
                        act.wait_ge(s_ready, s[1])
                    a.activation(zT[:, :], shared[:, :], ACT.Copy).then_inc(zT_ready, 1)
                elif kind == "hidden" and s[2] == 0:
                    f = s[1]
                    act.wait_ge(shared_filled, fills[s])
                    if f >= 2:
                        act.wait_ge(shared_filled, fills[("down", f - 2)])
                    for c in range(FC):
                        last = a.activation(hT[:, f % 2, c, :], shared[:, c * P:(c + 1) * P], ACT.Relu,
                                            bias=pair[:, f % WB, T_B1 + c:T_B1 + c + 1])
                    last.then_inc(hid_ready[0], 1)
                elif kind == "gate":
                    for b in range(B):
                        act.wait_ge(gathered[b], 16 * C)
                    for q in range(GATE_STEPS):
                        part = yg[:, NT // GATE_STEPS * q:NT // GATE_STEPS * (q + 1), :]
                        a.activation(part, part, ACT.Silu, scale=0.5).then_inc(gate_ready, 1)

        @block.vector
        def _(dve):
            v = nc.vector
            chain = [0]

            def link(ins):
                chain[0] += 1
                ins.then_inc(dve_chain, 1)
                dve.wait_ge(dve_chain, chain[0])

            v.memset(ones_bf[:, :], 1.0)
            v.memset(zeros, 0.0)
            link(v.memset(va[:, :, :, :, HD:VW], 0.0))
            v.memset(va[:, :, :, :, HD:HD + 1], 1.0).then_inc(dve_consts, 1)

            def fold():
                dve.wait_ge(lam_dots, 64)
                link(v.tensor_tensor(lam_prod[:, :, :], lams[:, 0:2, :], lams[:, 2:4, :], ALU.mult))
                v.tensor_reduce(lam_dot[:, :], lam_prod[:, :, :], AX.X, ALU.add).then_inc(lam_dots, 1)
                dve.wait_ge(lam_exps, 1)
                link(v.tensor_tensor(neg_lam[:, :], lam_exp[:, 1:2], lam_exp[:, 0:1], ALU.subtract))
                link(v.tensor_scalar(neg_lam[:, :], neg_lam[:, :], -LAM_INIT, None, ALU.add))
                dve.wait_ge(small_loaded, 16 * SMALL)
                w = HALF * HD
                v.scalar_tensor_tensor(wv_eff[:, :], wv_sb[:, w:2 * w], neg_lam[:, 0:1], wv_sb[:, 0:w],
                                       ALU.mult, ALU.add)
                v.scalar_tensor_tensor(bv_eff[:, :], bv_sb[:, w:2 * w], neg_lam[:, 0:1], bv_sb[:, 0:w],
                                       ALU.mult, ALU.add)
                link(v.tensor_scalar(wo_eff[:, :], wo_sb[:, :], lnw_sb[:, 0:1], OUT_SCALE, ALU.mult, ALU.mult))
                dve.wait_ge(consts_ready, 1)
                v.tensor_copy(ident_bf[:, :], ident[:, :])
                v.tensor_scalar(lnb_wide[:, :], ones[:, :], lnb_sb[:, 0:1], OUT_SCALE,
                                ALU.mult, ALU.mult).then_inc(folded, 1)

            def build_table():
                dve.wait_ge(expert_loaded, 16 * 6)
                tab = table[:, :].rearrange("p (e w) -> p e w", e=EXP + 1)
                v.tensor_tensor(tab[:, 0:EXP, T_B2:T_B2 + D], tab[:, 0:EXP, T_B2:T_B2 + D],
                                tab[:, 1:EXP + 1, T_B2:T_B2 + D], ALU.add).then_inc(table_ready, 1)

            def count_groups():
                dve.wait_ge(xn_ready, B)
                dve.wait_ge(iota_ready, 1)
                link(v.tensor_tensor(v01[:, :], xn[:, :, 0], xn[:, :, 1], ALU.add))
                link(v.scalar_tensor_tensor(v_abs[:, :], v01[:, :], -1.0, v01[:, :], ALU.mult, ALU.max))
                c3 = cmp[:, 0:NT * 15].rearrange("p (t k) -> p t k", k=15)
                link(v.tensor_tensor(c3, v_abs[:, :].unsqueeze(2).to_broadcast([P, NT, 15]),
                                     iota[:, 1:16].unsqueeze(1).to_broadcast([P, NT, 15]), ALU.is_ge))
                link(v.tensor_reduce(n_abs[:, :], c3, AX.X, ALU.add))
                link(v.tensor_scalar(sign[:, :], v01[:, :], 0.0, 2.0, ALU.is_ge, ALU.mult))
                link(v.scalar_tensor_tensor(h[:, :], sign[:, :], -1.0, n_abs[:, :], ALU.add, ALU.mult))
                v.tensor_scalar(wrap[:, 0, :], h[:, :], 0.0, 8.0, ALU.is_lt, ALU.mult)
                v.tensor_scalar(wrap[:, 1, :], h[:, :], -8.0, 8.0, ALU.is_lt, ALU.mult)
                link(v.tensor_scalar(wrap[:, 2, :], h[:, :], 8.0, -8.0, ALU.is_ge, ALU.mult))
                for i in range(3):
                    link(v.tensor_tensor(h[:, :], h[:, :], wrap[:, i, :], ALU.add))
                link(v.tensor_tensor(onehot[:, :, :], h[:, :].unsqueeze(1).to_broadcast([P, EXP, NT]),
                                     iota[:, 0:EXP].unsqueeze(2).to_broadcast([P, EXP, NT]), ALU.is_equal))
                v.tensor_reduce(count[:, :], onehot[:, :, :], AX.X, ALU.add).then_inc(count_ready, 1)
                flat = work[:, 768:1024]
                link(v.tensor_tensor_scan(flat, work[:, 512:768], zeros,
                                          0.0, ALU.add, ALU.add))
                v.tensor_tensor(seen[:, :, :], seen[:, :, :], onehot[:, :, :], ALU.subtract).then_inc(seen_ready, 1)

            def make_slots(fill, shared):
                dve.wait_ge(shared_filled, fill)
                c2 = cmp[:, 0:EXP * NT].rearrange("p (e k) -> p e k", k=NT)
                link(v.tensor_scalar(tile_base[:, :], shared[:, EXP:2 * EXP], 1.0 / P, None, ALU.mult))
                link(v.tensor_tensor(c2, tile_base[:, :].unsqueeze(2).to_broadcast([P, EXP, NT]),
                                     iota[:, 0:NT].unsqueeze(1).to_broadcast([P, EXP, NT]), ALU.is_gt))
                link(v.tensor_reduce(tiles_of[:, :], c2, AX.X, ALU.add))
                link(v.tensor_tensor_scan(tile_end[:, :], tiles_of[:, :], zeros[:, 0:EXP], 0.0, ALU.add, ALU.add))
                link(v.tensor_tensor(tile_base[:, :], tile_end[:, :], tiles_of[:, :], ALU.subtract))
                v.scalar_tensor_tensor(base[:, :], tile_base[:, :], float(P), shared[:, 0:EXP],
                                       ALU.mult, ALU.add).then_inc(counts_read, 1)
                dve.wait_ge(counts_read, 1)
                dve.wait_ge(seen_ready, 1)
                link(v.tensor_tensor(base[:, :], base[:, :], seen[:, :, 0], ALU.subtract))
                link(v.tensor_tensor(seen[:, :, :], seen[:, :, :],
                                     base[:, :].unsqueeze(2).to_broadcast([P, EXP, NT]), ALU.add))
                link(v.tensor_tensor(seen[:, :, :], seen[:, :, :], onehot[:, :, :], ALU.mult))
                link(v.tensor_reduce(slot_f[:, :], seen[:, :, :].rearrange("p e t -> p t e"), AX.X, ALU.add))
                v.tensor_copy(slot[:, :], slot_f[:, :]).then_inc(slots_ready, 1)

            def tile_experts():
                c1 = cmp[:, 0:FT * (EXP - 1)].rearrange("p (f e) -> p f e", e=EXP - 1)
                link(v.tensor_tensor(c1, iota[:, 0:FT].unsqueeze(2).to_broadcast([P, FT, EXP - 1]),
                                     tile_base[:, 1:EXP].unsqueeze(1).to_broadcast([P, FT, EXP - 1]), ALU.is_ge))
                link(v.tensor_reduce(texp_f[:, :], c1, AX.X, ALU.add))
                v.tensor_copy(texp[:, :], texp_f[:, :]).then_inc(texp_ready, 1)

            for s in steps:
                kind = s[0]
                shared = ring[uses[s] % RING] if s in uses else None
                if kind == "stats":
                    b = s[1]
                    dve.wait_ge(x_loaded[b], 16)
                    if b >= 1:
                        dve.wait_ge(stats_ready, b)
                    if b >= 2:
                        dve.wait_ge(rstd_ready, b - 1)
                    for c in range(C):
                        last = v.bn_stats(stats[:, c, :], xin[:, C * b + c, :])
                    link(last)
                    for c in range(C):
                        last = v.bn_aggr(mv[:, b % 2, c, :], stats[:, c, :])
                    last.then_inc(stats_ready, 1)
                elif kind == "transpose_x":
                    b = s[1]
                    dve.wait_ge(shared_filled, fills[s])
                    if b >= 2:
                        dve.wait_ge(shared_filled, fills[("values", b - 2)])
                    v.tensor_copy(xT[:, b % 2, :], shared[:, :]).then_inc(xT_ready, 1)
                elif kind == "project":
                    b, i = s[1:]
                    dve.wait_ge(high_ready, 2 * b + i + 1)
                    if b >= 1:
                        dve.wait_ge(low_ready, 2 * b + i - 1)
                    v.scalar_tensor_tensor(rest[:, i, :], shared[:, :], qk_bias[:, i:i + 1], parts[:, i, 0, :],
                                           ALU.add, ALU.subtract).then_inc(rest_ready, 1)
                elif kind == "split" and s[1] < 2:
                    b, i = s[1:]
                    dve.wait_ge(mid_ready, 2 * b + i + 1)
                    v.tensor_tensor(parts[:, i, 2, :], rest[:, i, :], parts[:, i, 1, :],
                                    ALU.subtract).then_inc(low_ready, 1)
                elif kind == "values":
                    b = s[1]
                    dve.wait_ge(shared_filled, fills[s])
                    if b >= 2:
                        dve.wait_ge(pv_done, 8 * (b - 1))
                    w = HALF * HD
                    v.tensor_tensor(va[:, b % 2, :, :, 0:HD],
                                    shared[:, 0:C * w].rearrange("p (c i d) -> p c i d", c=C, d=HD),
                                    bv_eff[:, :].rearrange("p (i d) -> p i d", d=HD).unsqueeze(1)
                                    .to_broadcast([P, C, HALF, HD]), ALU.add).then_inc(va_ready, 1)
                elif kind == "score":
                    n = s[1]
                    b, col = divmod(n, HEADS * C)
                    dve.wait_ge(score_filled, n + 1)
                    if col == 0 and b >= 2:
                        dve.wait_ge(max_split, 2 * (b - 1))
                    v.tensor_reduce(neg_max[:, b % 2, col:col + 1], score_bank[n % 2][:, :], AX.X, ALU.max,
                                    negate=True).then_inc(max_taken, 1)
                elif kind == "split_max":
                    grp = s[1]
                    b, g2 = divmod(grp, 2)
                    dve.wait_ge(max_taken, 16 * (grp + 1))
                    if grp >= 2:
                        dve.wait_ge(shared_filled, fills[("turn_max", grp - 2)])
                    part = [max_parts[:, g2, j, :] for j in range(PARTS)]
                    whole = neg_max[:, b % 2, 16 * g2:16 * g2 + 16]
                    link(v.tensor_copy(part[0], whole))
                    link(v.tensor_tensor(max_rest[:, g2, :], whole, part[0], ALU.subtract))
                    link(v.tensor_copy(part[1], max_rest[:, g2, :]))
                    v.tensor_tensor(part[2], max_rest[:, g2, :], part[1], ALU.subtract).then_inc(max_split, 1)
                elif kind == "turn_max":
                    grp = s[1]
                    dve.wait_ge(shared_filled, fills[s])
                    if grp >= 2:
                        dve.wait_ge(max_stacked, 16 * (grp - 1))
                    v.tensor_copy(max_rows[:, grp % 2, :], shared[0:PARTS * 16, 0:P // 2].bitcast(BF16)).then_inc(max_turned, 1)
                elif kind == "b1":
                    dve.wait_ge(shared_filled, fills[s])
                    tab = table[:, :].rearrange("p (e w) -> p e w", e=EXP + 1)
                    rows = shared[:, 0:EXP * FC].rearrange("p (e c) -> p e c", c=FC)
                    v.tensor_copy(tab[:, 0:EXP, T_B1:T_B1 + FC], rows)
                    v.tensor_copy(tab[:, EXP, T_B1:T_B1 + FC], rows[:, 0, :]).then_inc(b1_ready, 1)
                elif kind == "turn_o":
                    grp = s[1]
                    b, g2 = divmod(grp, 2)
                    dve.wait_ge(shared_filled, fills[s])
                    if grp >= 4:
                        dve.wait_ge(z_ready, b - 1)
                    if grp >= 1:
                        dve.wait_ge(attn_ready, grp)
                    o4 = shared[:, :].rearrange("p (c i w) -> p c i w", c=C, w=VW)
                    link(v.reciprocal(inv_sum[:, :], shared[:, :].rearrange("p (n w) -> p n w", w=VW)[:, :, HD]))
                    v.tensor_tensor(attn[:, b % 2, :, g2 * HALF * HD:(g2 + 1) * HALF * HD]
                                    .rearrange("p c (i d) -> p c i d", d=HD), o4[:, :, :, 0:HD],
                                    inv_sum[:, :].rearrange("p (c i) -> p c i", c=C).unsqueeze(3)
                                    .to_broadcast([P, C, HALF, HD]), ALU.mult).then_inc(attn_ready, 1)
                elif kind == "norm_o":
                    b = s[1]
                    dve.wait_ge(attn_ready, 2 * b + 2)
                    if b >= 1:
                        dve.wait_ge(z_ready, b)
                    for c in range(C):
                        last = v.bn_stats(stats_o[:, c, :], attn[:, b % 2, c, :])
                    link(last)
                    for c in range(C):
                        last = v.bn_aggr(mv_o[:, c, :], stats_o[:, c, :])
                    last.then_inc(stats_o_ready, 1)
                elif kind == "scale_o":
                    b = s[1]
                    dve.wait_ge(rstd_o_ready, b + 1)
                    if b >= 1:
                        dve.wait_ge(shared_filled, fills[("turn_z", b - 1)])
                    for c in range(C):
                        last = v.tensor_scalar(z[:, c, :], attn[:, b % 2, c, :], rstd_o[:, c:c + 1],
                                               shift_o[:, c:c + 1], ALU.mult, ALU.add)
                    last.then_inc(z_ready, 1)
                elif kind == "project_o":
                    b = s[1]
                    dve.wait_ge(shared_filled, fills[s])
                    dve.wait_ge(xn_ready, b + 1)
                    if b == 0:
                        dve.wait_ge(bias_ready, 1)
                    v.tensor_tensor(s_sb[:, C * b:C * b + C, :], shared[:, :].rearrange("p (c n) -> p c n", c=C),
                                    bo_eff[:, :].unsqueeze(1).to_broadcast([P, C, D]), ALU.add).then_inc(s_ready, 1)
                elif kind == "fold_qk":
                    dve.wait_ge(qk_loaded, 16 * 4)
                    for i, w in enumerate((wq_sb, wk_sb)):
                        last = v.tensor_copy(wqk[:, i, :].rearrange("p (d h) -> p h d", d=HD),
                                             w[:, :].rearrange("p (h d) -> p h d", d=HD))
                    last.then_inc(qk_folded, 1)
                elif kind == "fold":
                    fold()
                elif kind == "bias_o":
                    dve.wait_ge(shared_filled, fills[s])
                    v.tensor_tensor(bo_eff[:, :], shared[:, 0:D], bo_sb[:, :], ALU.add).then_inc(bias_ready, 1)
                elif kind == "table":
                    build_table()
                elif kind == "route":
                    if s[1] == 0:
                        count_groups()
                    elif s[1] == 1:
                        make_slots(fills[s], shared)
                    else:
                        tile_experts()
                elif kind == "turn_tile":
                    f = s[1]
                    dve.wait_ge(shared_filled, fills[s])
                    if f >= 2:
                        dve.wait_ge(shared_filled, fills[("hidden", f - 2, 1)])
                    v.tensor_copy(xsT[:, f % 2, :], shared[:, 0:P]).then_inc(xsT_ready, 1)
                elif kind == "hidden" and s[2] == 1:
                    f = s[1]
                    dve.wait_ge(shared_filled, fills[s])
                    if f >= 2:
                        dve.wait_ge(shared_filled, fills[("down", f - 2)])
                    for c in range(FC):
                        last = v.tensor_scalar(hT[:, f % 2, FC + c, :], shared[:, c * P:(c + 1) * P],
                                               pair[:, f % WB, TW + T_B1 + c:TW + T_B1 + c + 1], 0.0,
                                               ALU.add, ALU.max)
                    last.then_inc(hid_ready[1], 1)
                elif kind == "down":
                    f = s[1]
                    dve.wait_ge(shared_filled, fills[s])
                    if f >= 2:
                        dve.wait_ge(y_stored[f % 2], 16 * (f // 2))
                    v.tensor_tensor(y_sb[:, f % 2, :], shared[:, 0:D], pair[:, f % WB, T_B2:T_B2 + D],
                                    ALU.add).then_inc(y_ready, 1)
                elif kind == "finish" and s[1] in DVE_FINISH:
                    finish(dve, v, s[1], link).then_inc(out_ready, 1)

        @block.tensor
        def _(pe):
            t = nc.tensor

            def free(use):
                if use >= RING:
                    pe.wait_ge(*reader[use - RING])

            reader = {}
            for s, use in uses.items():
                kind = s[0]
                reader[use] = {
                    "transpose_x": lambda: (xT_ready, s[1] + 1),
                    "project": lambda: (rest_ready, 2 * s[1] + s[2] + 1),
                    "values": lambda: (va_ready, s[1] + 1),
                    "turn_max": lambda: (max_turned, s[1] + 1),
                    "b1": lambda: (b1_ready, 1),
                    "turn_o": lambda: (attn_ready, s[1] + 1),
                    "turn_z": lambda: (zT_ready, s[1] + 1),
                    "project_o": lambda: (s_ready, s[1] + 1),
                    "bias_o": lambda: (bias_ready, 1),
                    "route": lambda: (counts_read, 1),
                    "turn_tile": lambda: (xsT_ready, s[1] + 1),
                    "down_first": lambda: (y_ready, s[1] + 1),
                    "down": lambda: (y_ready, s[1] + 1),
                    "hidden": lambda: (hid_ready[s[2]], s[1] + 1),
                }[kind]()

            pe.wait_ge(consts_ready, 1)
            for s in steps:
                kind = s[0]
                shared = ring[uses[s] % RING] if s in uses else None
                if kind == "transpose_x":
                    b = s[1]
                    pe.wait_ge(xn_ready, b + 1)
                    free(uses[s])
                    for c in range(C):
                        last = t.transpose(shared[:, c * P:(c + 1) * P], xn[:, C * b + c, :], ident[:, :])
                    last.then_inc(shared_filled, 1)
                elif kind == "bias_o":
                    pe.wait_ge(folded, 1)
                    free(uses[s])
                    t.matmul(shared[:, 0:D], lnb_wide[:, :], wo_sb[:, :], start=True, stop=True).then_inc(shared_filled, 1)
                elif kind == "project":
                    b, i = s[1:]
                    if b == 0 and i == 0:
                        pe.wait_ge(qk_folded, 1)
                    if i == 0:
                        pe.wait_ge(xT_ready, b + 1)
                    free(uses[s])
                    t.matmul(shared[:, :], wqk[:, i, :], xT[:, b % 2, :], start=True, stop=True).then_inc(shared_filled, 1)
                elif kind == "values":
                    b = s[1]
                    if b == 0:
                        pe.wait_ge(folded, 1)
                    free(uses[s])
                    w = HALF * HD
                    for c in range(C):
                        last = t.matmul(shared[:, c * w:(c + 1) * w], xT[:, b % 2, c * P:(c + 1) * P], wv_eff[:, :],
                                        start=True, stop=True)
                    last.then_inc(shared_filled, 1)
                elif kind == "score":
                    n = s[1]
                    b, col = divmod(n, HEADS * C)
                    hh, c = divmod(col, C)
                    if col == 0:
                        pe.wait_ge(stacked[b % STK], 12 * 16 * (b // STK + 1))
                    if n >= 2:
                        pe.wait_ge(max_taken, n - 1)
                    t.matmul(score_bank[n % 2][:, :], qs[0:MAX_ROW, b % STK, hh, c * P:(c + 1) * P],
                             ks[0:MAX_ROW, b % STK, hh, :], start=True, stop=True).then_inc(score_filled, 1)
                elif kind == "turn_max":
                    grp = s[1]
                    pe.wait_ge(max_split, grp + 1)
                    free(uses[s])
                    t.transpose(shared[0:PARTS * 16, 0:P // 2].bitcast(BF16),
                                max_parts[:, grp % 2, :, :].rearrange("p j n -> p (j n)"),
                                ident_bf[:, :]).then_inc(shared_filled, 1)
                elif kind == "b1":
                    pe.wait_ge(b1_loaded, 16)
                    free(uses[s])
                    t.transpose(shared[:, 0:EXP * FC], b1_rows[:, :], ident[0:EXP * FC, 0:EXP * FC]).then_inc(shared_filled, 1)
                elif kind == "exp":
                    n = s[1]
                    b, r = divmod(n, HEADS * C)
                    g2, r = divmod(r, C * HALF)
                    kc, i = divmod(r, HALF)
                    hh = g2 * HALF + i
                    if n % 16 == 0:
                        pe.wait_ge(max_stacked, 16 * (n // 16 + 1))
                        if n == 0:
                            pe.wait_ge(ones_stacked, 16 * STK)
                    if n >= 2:
                        pe.wait_ge(exp_done, n - 1)
                    t.matmul(exp_bank[n % 2][:, :], ks[0:KROWS, b % STK, hh, kc * P:(kc + 1) * P],
                             qs[0:KROWS, b % STK, hh, :], start=True, stop=True).then_inc(exp_filled, 1)
                elif kind == "pv":
                    n4 = s[1]
                    grp, kc = divmod(n4, C)
                    b = grp // 2
                    pe.wait_ge(exp_done, 4 * n4 + 4)
                    if n4 % (2 * C) == 0:
                        pe.wait_ge(va_ready, b + 1)
                    if kc == 0 and grp >= 1:
                        pe.wait_ge(o_copied, grp)
                    for i in range(HALF):
                        last = t.matmul(pv_bank[VW * i:VW * (i + 1), :], va[:, b % 2, kc, i, :],
                                        probs[:, (4 * n4 + i) % PR, :], start=(kc == 0), stop=(kc == C - 1))
                    last.then_inc(pv_done, 1)
                elif kind == "turn_o":
                    grp = s[1]
                    pe.wait_ge(o_copied, grp + 1)
                    free(uses[s])
                    for c in range(C):
                        last = t.transpose(shared[:, c * P:(c + 1) * P], oT[:, grp % 2, c * P:(c + 1) * P], ident[:, :])
                    last.then_inc(shared_filled, 1)
                elif kind == "turn_z":
                    pe.wait_ge(z_ready, s[1] + 1)
                    free(uses[s])
                    for c in range(C):
                        last = t.transpose(shared[:, c * P:(c + 1) * P], z[:, c, :], ident[:, :])
                    last.then_inc(shared_filled, 1)
                elif kind == "project_o":
                    pe.wait_ge(zT_ready, s[1] + 1)
                    free(uses[s])
                    for c in range(C):
                        last = t.matmul(shared[:, c * D:(c + 1) * D], zT[:, c * P:(c + 1) * P], wo_eff[:, :],
                                        start=True, stop=True)
                    last.then_inc(shared_filled, 1)
                elif kind == "route" and s[1] == 1:
                    pe.wait_ge(count_ready, 1)
                    free(uses[s])
                    t.matmul(shared[:, 0:EXP], before[:, :], count[:, :], start=True, stop=True)
                    t.matmul(shared[:, EXP:2 * EXP], ones[:, :], count[:, :], start=True, stop=True).then_inc(shared_filled, 1)
                elif kind == "turn_tile":
                    f = s[1]
                    pe.wait_ge(tile_loaded[f % 2], 16 * (f // 2 + 1))
                    free(uses[s])
                    t.transpose(shared[:, 0:P], xs[:, f % 2, :], ident[:, :]).then_inc(shared_filled, 1)
                elif kind == "hidden":
                    f, j = s[1:]
                    if j == 0:
                        pe.wait_ge(pair_loaded[f % WB], 16 * (f // WB + 1))
                        pe.wait_ge(xsT_ready, f + 1)
                    free(uses[s])
                    for c in range(FC):
                        o = j * TW + T_W1 + c * P
                        last = t.matmul(shared[:, c * P:(c + 1) * P], pair[:, f % WB, o:o + P], xsT[:, f % 2, :],
                                        start=True, stop=True)
                    last.then_inc(shared_filled, 1)
                elif kind in ("down_first", "down"):
                    f = s[1]
                    half = int(kind == "down")
                    ks_of = range(FC * half, FC * (half + 1))
                    e = pe.value_load(texp[0:1, f:f + 1], min_val=0, max_val=EXP - 1)
                    w2_at = [pe.snap(e * FF + k * D) for k in ks_of]
                    pe.wait_ge(hid_ready[half], f + 1)
                    if half == 0:
                        free(uses[s])
                    for k in ks_of:
                        last = t.matmul(shared[:, 0:D], hT[:, f % 2, k, :], w2_sb[:, bass.ds(w2_at[k - FC * half], D)],
                                        start=(k == 0), stop=(k == 2 * FC - 1))
                    if half == 1:
                        last.then_inc(shared_filled, 1)


_INS = ["L0_attn_hidden_states", "L0_attn_Wq", "L0_attn_bq", "L0_attn_Wk", "L0_attn_bk", "L0_attn_Wv", "L0_attn_bv",
        "L0_attn_Wo", "L0_attn_bo", "L0_attn_lambda_q1", "L0_attn_lambda_k1", "L0_attn_lambda_q2",
        "L0_attn_lambda_k2", "L0_attn_ln_w", "L0_attn_ln_b", "L0_ffn_W1", "L0_ffn_b1", "L0_ffn_W2", "L0_ffn_b2"]
_OUTS = [((8, 512, 128), "float32")]


def kernel(**inputs):
    import numpy as _np
    import concourse.bacc as _bacc
    from concourse import mybir as _mybir
    from concourse.bass_utils import run_bass_kernel_spmd as _run

    nc = _bacc.Bacc("TRN2", target_bir_lowering=False, num_devices=1)
    arrays, args = {}, []
    for name in _INS:
        a = _np.ascontiguousarray(inputs[name])
        arrays[f"in_{name}_dram"] = a
        args.append(nc.dram_tensor(f"in_{name}_dram", a.shape, _mybir.dt.from_np(a.dtype), kind="ExternalInput").ap())
    for i, (shape, dtype) in enumerate(_OUTS):
        dt = _mybir.dt.from_np(_np.dtype(dtype))
        args.append(nc.dram_tensor(f"out_{i}_dram", shape, dt, kind="ExternalOutput").ap())
    gated_attention_moe(nc, *args)
    r = _run(nc, [arrays], core_ids=[0])
    return r.results[0]["out_0_dram"]
```
